# Optimizing a Trainium2 kernel written in Bass

```python
import numpy as np
import jax
import jax.numpy as jnp

def _softmax(x, axis=-1):
    return jax.nn.softmax(x, axis=axis)

def _gelu(x):
    return jax.nn.gelu(x, approximate=True)

def _silu(x):
    return jax.nn.silu(x)

def _sigmoid(x):
    return jax.nn.sigmoid(x)

def _layernorm(x, axis=-1, eps=1e-05):
    m = jnp.mean(x, axis=axis, keepdims=True)
    v = jnp.var(x, axis=axis, keepdims=True)
    return (x - m) / jnp.sqrt(v + eps)

def _scatter_add(tgt, idx, src, axis=0):
    return tgt.at[idx].add(src)

def _segment_sum(src, seg, n):
    return jax.ops.segment_sum(src, seg, n)
kernel_name = 'mk_flamingo_gated_d1_seqx_r4_973ce6'

def setup_inputs(seed: int=0):
    np.random.seed(seed)
    _w = jnp.asarray

    def _rec_inputs():
        import jax
        import jax.numpy as jnp
        _rk = jax.random.key(seed)
        x = -0.0002928 + 1 * jax.random.normal(jax.random.fold_in(_rk, 1), (32, 256, 256), jnp.float32)
        _lenS = 256 - jax.random.randint(jax.random.fold_in(_rk, 7), (32,), 0, max(1, 256 // 4) + 1, jnp.int32)
        _lenS2 = 256 - jax.random.randint(jax.random.fold_in(_rk, 8), (32,), 0, max(1, 256 // 4) + 1, jnp.int32)
        _ctx_1024P = jax.random.normal(jax.random.fold_in(_rk, 11), (32, 16, 256), jnp.float32)
        _ctx_1024c = jax.random.dirichlet(jax.random.fold_in(_rk, 511), 0.3 * jnp.ones((16,), jnp.float32), (32, 256))
        _ctx_1024t = jnp.einsum('bsk,bkd->bsd', _ctx_1024c, _ctx_1024P)
        _ctx_1024t = _ctx_1024t * jax.lax.rsqrt(jnp.mean(jnp.square(_ctx_1024t)) + 1e-12) * 0.953939
        ctx_1024 = -1.39393e-06 + 0.999914 * (_ctx_1024t + 0.3 * jax.random.normal(jax.random.fold_in(_rk, 611), (32, 256, 256), jnp.float32))
        _g = jax.random.normal(jax.random.fold_in(_rk, 9001), (2, 1), jnp.float32)
        _g = jnp.sign(_g) * jnp.maximum(jnp.abs(_g), 1.0) + (_g == 0) * 1.0
        g_xattn = _g[0]
        g_ffn = _g[1]
        return (x, ctx_1024, g_xattn, g_ffn)
    x, ctx_1024, g_xattn, g_ffn = _rec_inputs()

    def _L0_xattn_setup():
        import jax, jax.numpy as jnp
        import numpy as np
        import math
        NUM_HEADS = 16
        TOPK = 64
        EMBED = 256

        def _topk_attention(Q, K, V, topk):
            d = Q.shape[-1]
            scores = jnp.einsum('bhqd,bhkd->bhqk', Q, K) / jnp.sqrt(jnp.asarray(d, Q.dtype))
            topk_scores, topk_idx = jax.lax.top_k(scores, topk)
            probs = jax.nn.softmax(topk_scores, axis=-1)
            gather = jax.vmap(jax.vmap(lambda Vbh, idx: Vbh[idx]))
            sel = gather(V, topk_idx)
            return jnp.einsum('bhqk,bhqkd->bhqd', probs, sel)
        key = jax.random.key(seed)
        ks = jax.random.split(key, 11)
        b, s, e = (2, 512, EMBED)
        scale = 1.0 / math.sqrt(e)
        inp = {'q': jax.random.normal(ks[0], (b, s, e), dtype=jnp.float32), 'k': jax.random.normal(ks[1], (b, s, e), dtype=jnp.float32), 'v': jax.random.normal(ks[2], (b, s, e), dtype=jnp.float32), 'Wq': jax.random.normal(ks[3], (e, e), dtype=jnp.float32) * scale, 'bq': jnp.zeros((e,), dtype=jnp.float32), 'Wk': jax.random.normal(ks[4], (e, e), dtype=jnp.float32) * scale, 'bk': jnp.zeros((e,), dtype=jnp.float32), 'Wv': jax.random.normal(ks[5], (e, e), dtype=jnp.float32) * scale, 'bv': jnp.zeros((e,), dtype=jnp.float32), 'Wo': jax.random.normal(ks[6], (e, e), dtype=jnp.float32) * scale, 'bo': jnp.zeros((e,), dtype=jnp.float32)}
        return inp
    _L0_xattn_all = _L0_xattn_setup()
    _L0_xattn_in = {k: v for k, v in _L0_xattn_all.items() if k in ('Wq', 'bq', 'Wk', 'bk', 'Wv', 'bv', 'Wo', 'bo')}
    del _L0_xattn_all

    def _L0_ffn_setup():
        import jax, jax.numpy as jnp
        import numpy as np
        FEATURES = 256
        D_IN = 256

        def fp8_gemm_optimized(x, input_scale, kernel, kernel_scale):
            s_in = input_scale[0]
            s_k = kernel_scale[0]
            x_q = (x.astype(jnp.float32) / s_in).astype(jnp.float8_e4m3fn)
            k_q = (kernel.astype(jnp.float32) / s_k).astype(jnp.float8_e4m3fn)
            y = jnp.dot(x_q.astype(jnp.float32), k_q.astype(jnp.float32), preferred_element_type=jnp.float32)
            return y * (s_in * s_k)
        key = jax.random.key(seed)
        kx, kk, kb = jax.random.split(key, 3)
        x = jax.random.normal(kx, (4, 2048, D_IN), dtype=jnp.float32)
        limit = np.sqrt(6.0 / (D_IN + FEATURES)).astype(np.float32)
        kernel = jax.random.uniform(kk, (D_IN, FEATURES), dtype=jnp.float32, minval=-limit, maxval=limit).astype(jnp.bfloat16)
        input_scale = jnp.ones((1,), dtype=jnp.float32)
        kernel_scale = jnp.ones((1,), dtype=jnp.float32)
        bias = jnp.zeros((FEATURES,), dtype=jnp.bfloat16)
        return {'x': x, 'kernel': kernel, 'input_scale': input_scale, 'kernel_scale': kernel_scale, 'bias': bias}
    _L0_ffn_all = _L0_ffn_setup()
    _L0_ffn_in = {k: v for k, v in _L0_ffn_all.items() if k in ('kernel', 'input_scale', 'kernel_scale', 'bias')}
    del _L0_ffn_all
    return {'x': x, 'ctx_1024': ctx_1024, 'g_xattn': g_xattn, 'g_ffn': g_ffn, 'L0_xattn_Wq': _L0_xattn_in['Wq'], 'L0_xattn_bq': _L0_xattn_in['bq'], 'L0_xattn_Wk': _L0_xattn_in['Wk'], 'L0_xattn_bk': _L0_xattn_in['bk'], 'L0_xattn_Wv': _L0_xattn_in['Wv'], 'L0_xattn_bv': _L0_xattn_in['bv'], 'L0_xattn_Wo': _L0_xattn_in['Wo'], 'L0_xattn_bo': _L0_xattn_in['bo'], 'L0_ffn_kernel': _L0_ffn_in['kernel'], 'L0_ffn_input_scale': _L0_ffn_in['input_scale'], 'L0_ffn_kernel_scale': _L0_ffn_in['kernel_scale'], 'L0_ffn_bias': _L0_ffn_in['bias']}

def reference(x, ctx_1024, g_xattn, g_ffn, L0_xattn_Wq, L0_xattn_bq, L0_xattn_Wk, L0_xattn_bk, L0_xattn_Wv, L0_xattn_bv, L0_xattn_Wo, L0_xattn_bo, L0_ffn_kernel, L0_ffn_input_scale, L0_ffn_kernel_scale, L0_ffn_bias):
    import jax
    import jax.numpy as jnp

    def _L0_xattn_ref(q, k, v, Wq, bq, Wk, bk, Wv, bv, Wo, bo):
        import jax, jax.numpy as jnp
        import numpy as np
        import math
        NUM_HEADS = 16
        TOPK = 64
        EMBED = 256

        def _topk_attention(Q, K, V, topk):
            d = Q.shape[-1]
            scores = jnp.einsum('bhqd,bhkd->bhqk', Q, K) / jnp.sqrt(jnp.asarray(d, Q.dtype))
            topk_scores, topk_idx = jax.lax.top_k(scores, topk)
            probs = jax.nn.softmax(topk_scores, axis=-1)
            gather = jax.vmap(jax.vmap(lambda Vbh, idx: Vbh[idx]))
            sel = gather(V, topk_idx)
            return jnp.einsum('bhqk,bhqkd->bhqd', probs, sel)
        b, s, e = q.shape
        h = NUM_HEADS
        d = e // h
        Q = (q @ Wq.T + bq).reshape(b, h, s, d)
        K = (k @ Wk.T + bk).reshape(b, h, s, d)
        V = (v @ Wv.T + bv).reshape(b, h, s, d)
        attn = _topk_attention(Q, K, V, TOPK)
        out = attn.reshape(b, s, e)
        return out @ Wo.T + bo

    def _L0_ffn_ref(x, kernel, input_scale, kernel_scale, bias):
        import jax, jax.numpy as jnp
        import numpy as np
        FEATURES = 256
        D_IN = 256

        def fp8_gemm_optimized(x, input_scale, kernel, kernel_scale):
            s_in = input_scale[0]
            s_k = kernel_scale[0]
            x_q = (x.astype(jnp.float32) / s_in).astype(jnp.float8_e4m3fn)
            k_q = (kernel.astype(jnp.float32) / s_k).astype(jnp.float8_e4m3fn)
            y = jnp.dot(x_q.astype(jnp.float32), k_q.astype(jnp.float32), preferred_element_type=jnp.float32)
            return y * (s_in * s_k)
        dtype = jnp.bfloat16
        x = x.astype(dtype)
        orig_shape = x.shape
        x2 = x.reshape(-1, x.shape[-1])
        y = fp8_gemm_optimized(x2, input_scale, kernel, kernel_scale)
        y = y.astype(dtype) + bias
        return y.reshape(orig_shape[:-1] + (FEATURES,))
    x = x + jnp.tanh(g_xattn[0]) * _L0_xattn_ref(_layernorm(x, axis=-1), ctx_1024, ctx_1024, L0_xattn_Wq, L0_xattn_bq, L0_xattn_Wk, L0_xattn_bk, L0_xattn_Wv, L0_xattn_bv, L0_xattn_Wo, L0_xattn_bo)
    x = x + jnp.tanh(g_ffn[0]) * _L0_ffn_ref(_layernorm(x, axis=-1), L0_ffn_kernel, L0_ffn_input_scale, L0_ffn_kernel_scale, L0_ffn_bias)
    return x

_drawn_inputs = setup_inputs


def setup_inputs(seed=0):
    import zlib

    import numpy as np

    out = dict(_drawn_inputs(seed))
    spreads = {'L0_xattn_bq': (0.0, 0.1),
     'L0_xattn_bk': (0.0, 0.1),
     'L0_xattn_bv': (0.0, 0.1),
     'L0_xattn_bo': (0.0, 0.1),
     'L0_ffn_bias': (0.0, 0.1)}
    factors = {}
    for name, (base, spread) in spreads.items():
        noise = np.random.default_rng([zlib.crc32(name.encode()), seed]).standard_normal(out[name].shape)
        drawn = base * np.exp(spread * noise) if base else spread * noise
        out[name] = jnp.asarray(drawn.astype(out[name].dtype))
    for name, factor in factors.items():
        out[name] = (out[name] * factor).astype(out[name].dtype)
    return out
```

```python
from contextlib import ExitStack

import concourse.bass as bass
from concourse import mybir

ALU = mybir.AluOpType
ACT = mybir.ActivationFunctionType
AX = mybir.AxisListType
BF16 = mybir.dt.bfloat16
F32 = mybir.dt.float32
I32 = mybir.dt.int32

P = 128
NB = 32
TOK = 256
E = 256
D = 16
NJ = E // D
EC = E // P
TT = TOK // P
NTILE = NB * TT
TOPK = 64
GH = 8
GT = 2 * GH
RING = 4
SPLITS = 96
EPS = 1e-5
BIG = 3.0e38
Q_LEVELS = (0, 0, 1, 1, 0, 2)
K_LEVELS = (0, 1, 0, 1, 2, 0)
ROUNDS = TOPK // 8


def at(count):
    return max(count, 0) if isinstance(count, int) else count


def head_of(g, n):
    return 4 * (n % 4) + 2 * g + n // 4


def build(nc, x, ctx_in, g_x, g_f, Wq, bq, Wk, bk, Wv, bv, Wo, bo, fk, s_in, s_k, fb, out):
    with ExitStack() as stack:
        def sb(name, shape, dt=F32):
            return stack.enter_context(nc.sbuf_tensor(name, shape, dt))

        def ps(name, shape, dt=F32):
            return stack.enter_context(nc.psum_tensor(name, shape, dt))

        def sem(name):
            return stack.enter_context(nc.semaphore(name))

        x_in = sb("x_in", [P, TT, E])
        ctx_sb = sb("ctx_sb", [P, TT, E])
        xn_sb = sb("xn_sb", [P, TT, E])
        xT = sb("xT", [P, EC, TOK])
        cT = sb("cT", [P, EC, TOK])
        proj = [sb(f"proj{k}", [P, EC, TOK]) for k in range(3)]
        split = [[sb(f"split{k}_{lev}", [P, EC, TOK], BF16) for lev in range(3)] for k in range(2)]
        rest = sb("rest", [P, EC, TOK])
        q_rows = sb("q_rows", [SPLITS, NJ, TOK], BF16)
        qs = [sb(f"qs{p}", [SPLITS, NJ, NJ, D], BF16) for p in range(2)]
        ks = [sb(f"ks{p}", [SPLITS, NJ, TOK], BF16) for p in range(2)]
        vt = sb("vt", [D, NJ, P])
        vh = sb("vh", [D, GH, D, NJ])
        v_aug = [sb(f"v_aug{p}", [P, 2 * NJ, 2 * D]) for p in range(2)]
        score_sb = sb("score_sb", [P, RING, GT, TOK])
        mx = sb("mx", [P, RING, GT])
        nmx = sb("nmx", [P, RING, GT])
        thr = sb("thr", [P, RING, GT])
        work = sb("work", [P, 2, TOK])
        max8 = sb("max8", [P, 8])
        e_sb = sb("e_sb", [P, 2, 2, TOK])
        p_sb = sb("p_sb", [P, 2, 2, TOK])
        pT_sb = sb("pT_sb", [P, 2, 2 * TOK])
        o_sb = sb("o_sb", [P, NJ, 4 * D])
        attT = sb("attT", [P, EC, TOK])
        denT = sb("denT", [P, EC, TOK])
        recT = sb("recT", [P, EC, TOK])
        x_res = [sb(f"x_res{p}", [P, TT, E]) for p in range(2)]
        xb_sb = sb("xb_sb", [P, TT, E], BF16)
        y_sb = sb("y_sb", [P, TT, E])
        magic_sb = sb("magic_sb", [P, TT, E])
        ysum_sb = sb("ysum_sb", [P, TT, E])
        yabs_sb = sb("yabs_sb", [P, TT, E])
        xq_sb = sb("xq_sb", [P, TT, E], BF16)
        xqT = sb("xqT", [P, EC, TOK], BF16)
        f_sb = sb("f_sb", [P, TT, E], BF16)
        fbias_sb = sb("fbias_sb", [P, TT, E], BF16)
        w_raw = score_sb[:, RING - 1, 0:EC, :]
        wT = [sb(f"wT{k}", [P, EC, E]) for k in range(4)]
        b_col = sb("b_col", [P, 3, EC])
        bo_row = sb("bo_row", [P, E])
        fb_row = sb("fb_row", [P, E], BF16)
        fk_sb = sb("fk_sb", [P, EC, E], BF16)
        kq_sb = sb("kq_sb", [P, EC, E], BF16)
        gates = sb("gates", [P, 2])
        tg = sb("tg", [P, 2])
        scl = sb("scl", [P, 2])
        rscl = sb("rscl", [P, 2])
        oscl = sb("oscl", [P, 1])
        half_c = sb("half_c", [P, TT])
        ident = sb("ident", [P, P])
        identb = sb("identb", [P, P], BF16)
        stat6 = [sb(f"stat6_{k}", [P, TT, 6]) for k in range(2)]
        mv = [sb(f"mv_{k}", [P, TT, 2]) for k in range(2)]
        var = [sb(f"var_{k}", [P, TT]) for k in range(2)]
        rstd = [sb(f"rstd_{k}", [P, TT]) for k in range(2)]
        nmr = [sb(f"nmr_{k}", [P, TT]) for k in range(2)]
        rowmax = sb("rowmax", [P, TT])
        nanrow = sb("nanrow", [P, TT])

        ps_s = ps("ps_s", [P, 2, 512])
        ps_t = ps("ps_t", [P, 2, 512])
        ps_o = ps("ps_o", [P, 512])
        ps_a = ps("ps_a", [P, 512])
        ps_b = ps("ps_b", [P, 512])
        ps_x = ps("ps_x", [P, 512])
        ps_xb = ps_x[:, 0:TOK].bitcast(BF16)

        s_carrier = sem("register_waits_carried")
        s_w = sem("weights_loaded")
        s_small = sem("small_loaded")
        s_wps = sem("weight_in_psum")
        s_wev = sem("weight_evacuated")
        s_id = sem("constants_ready")
        s_tanh = sem("tanh_done")
        s_init = sem("setup_steps")
        s_kq = sem("kernel_quantised")
        s_x = sem("x_loaded")
        s_ctx = sem("ctx_loaded")
        s_mv = [sem(f"moments_ready{k}") for k in range(2)]
        s_bn = [sem(f"halves_ready{k}") for k in range(2)]
        s_ln = [sem(f"layernorm_steps{k}") for k in range(2)]
        s_xn = [sem(f"normalised{k}") for k in range(2)]
        s_sp = sem("split_steps")
        s_ft = sem("front_transposed")
        s_fe = sem("front_evacuated")
        s_fp = sem("projection_in_psum")
        s_pe = sem("projection_evacuated")
        s_qm = sem("queries_moved")
        s_km = sem("keys_moved")
        s_qh = sem("queries_by_head")
        s_vh = sem("values_by_head")
        s_fv = sem("value_projection_in_psum")
        s_pv = sem("value_projection_evacuated")
        s_v = sem("values_moved")
        s_vt = sem("values_transposed")
        s_va = sem("values_ready")
        s_S = sem("scores_in_psum")
        s_copied = sem("scores_copied")
        s_nm = sem("negated_max")
        s_step = sem("selection_steps")
        s_sel = sem("selected")
        s_exp = sem("exp_done")
        s_P = sem("probs_ready")
        s_T = sem("probs_transposed")
        s_PT = sem("probs_evacuated")
        s_PV = sem("values_mixed")
        s_O = sem("mixed_evacuated")
        s_Om = sem("mixed_moved")
        s_rec = sem("denominators_inverted")
        s_norm = sem("attention_normalised")
        s_xr = sem("residual_loaded")
        s_xg = sem("residual_prepared")
        s_op = sem("out_projected")
        s_x1 = sem("residual_updated")
        s_y = sem("scaled")
        s_yb = sem("exponent_taken")
        s_mg = sem("magic_ready")
        s_nan = sem("range_checked")
        s_add = sem("magic_added")
        s_q = sem("quantised")
        s_qt = sem("quantised_transposed")
        s_qe = sem("quantised_evacuated")
        s_fm = sem("ffn_in_psum")
        s_f = sem("ffn_evacuated")
        s_fb = sem("ffn_biased")
        s_res = sem("result_ready")
        s_out = sem("out_stored")

        def carry(eng):
            eng.sem_inc(s_carrier, 1)

        x_dram = x.rearrange("b (t p) e -> b p t e", p=P)
        ctx_dram = ctx_in.rearrange("b (t p) e -> b p t e", p=P)
        out_dram = out.rearrange("b (t p) e -> b p t e", p=P)
        QK_MOVES = len(Q_LEVELS) * 8 * 16
        V_MOVES = 8 * 16
        O_MOVES = 4 * 2 * 8 * 16

        def one(ap, b):
            return ap[bass.ds(b, 1)].rearrange("b p t e -> p (b t) e")

        def schedule(eng, batch):
            batch(0, 0, False, True, True, True)
            batch(1, 1, True, True, True, True)
            with eng.Fori(2, NB - 4, 2) as i:
                batch(i, 0, True, True, True, True)
                batch(i + 1, 1, True, True, True, True)
            for b in range(NB - 4, NB):
                batch(b, b % 2, True, b + 1 < NB, b + 2 < NB, b + 3 < NB)

        block = stack.enter_context(nc.Block())

        @block.sync
        def _(sp):
            def load_front(b):
                sp.wait_ge(s_xn[0], at(b))
                carry(sp)
                sp.dma_start(x_in[:], one(x_dram, b)).then_inc(s_x, 16)
                sp.wait_ge(s_ft, at(b))
                carry(sp)
                sp.dma_start(ctx_sb[:], one(ctx_dram, b)).then_inc(s_ctx, 16)

            def move_operands(b, p):
                sp.wait_ge(s_qh, at(b))
                carry(sp)
                for k, (dst, levels, moved) in enumerate(((q_rows, Q_LEVELS, s_qm), (ks[p], K_LEVELS, s_km))):
                    if k == 1:
                        sp.wait_ge(s_S, at(16 * (b - 1)))
                        carry(sp)
                    sp.wait_ge(s_sp, 10 * b + 5 * k + 5)
                    carry(sp)
                    for s, lev in enumerate(levels):
                        for jl in range(8):
                            d3 = dst[D * s:D * s + D].rearrange("d (c j) t -> d c j t", c=EC)[:, :, jl, :]
                            sp.dma_start(d3, split[k][lev][D * jl:D * jl + D]).then_inc(moved, 16)

            def move_values(b, half):
                sp.wait_ge(s_pv, b + 1)
                carry(sp)
                sp.wait_ge(s_vh, at(2 * b + half))
                carry(sp)
                for jl in range(8):
                    d3 = vt[:].rearrange("d (c j) t -> d c j t", c=EC)[:, :, jl, :]
                    sp.dma_start(d3, proj[2][D * jl:D * jl + D, :, half * P:half * P + P]).then_inc(s_v, 16)

            def move_out(b, p):
                sp.wait_ge(s_O, 4 * b + 4)
                carry(sp)
                sp.wait_ge(s_op, at(b))
                carry(sp)
                sp.wait_ge(s_rec, at(b))
                carry(sp)
                for c in range(4):
                    for base, dst in ((0, attT), (D, denT)):
                        src = o_sb[32 * c + base:32 * c + base + D].rearrange("d (c j) t -> d c j t", c=EC)
                        for jl in range(8):
                            sp.dma_start(dst[D * jl:D * jl + D, :, 64 * c:64 * c + 64], src[:, :, jl, :]).then_inc(s_Om, 16)

            for k, w in enumerate((Wq, Wk, Wv, Wo)):
                sp.wait_ge(s_wps, at(k))
                sp.dma_start(w_raw, w.rearrange("(c p) i -> p c i", p=P)).then_inc(s_w, 16)
                if k == 0:
                    load_front(0)
            for b in range(2):
                if b == 0:
                    load_front(1)
                move_operands(b, b)
                if b == 0:
                    move_values(0, 0)
                    move_values(0, 1)
            load_front(2)

            def batch(b, p, prev, one_more, two_more, three_more):
                sp.wait_ge(s_out, at(16 * (b - 1)))
                carry(sp)
                sp.dma_start(x_res[p][:], one(x_dram, b)).then_inc(s_xr, 16)
                if three_more:
                    load_front(b + 3)
                if one_more:
                    move_values(b + 1, 0)
                if two_more:
                    move_operands(b + 2, p)
                if one_more:
                    move_values(b + 1, 1)
                if prev:
                    sp.wait_ge(s_res, at(b))
                    carry(sp)
                    sp.dma_start(one(out_dram, b - 1), x_res[1 - p][:]).then_inc(s_out, 16)
                move_out(b, p)

            schedule(sp, batch)
            sp.wait_ge(s_res, NB)
            sp.dma_start(one(out_dram, NB - 1), x_res[1][:]).then_inc(s_out, 16)
            sp.wait_ge(s_out, 16 * NB)

        @block.gpsimd
        def _(pool):
            nc.gpsimd.memset(ident[:], 0.0).then_inc(s_id, 1)
            pool.wait_ge(s_id, 1)
            nc.gpsimd.affine_select(out=ident[:], in_=ident[:], compare_op=ALU.not_equal, fill=1.0, base=0,
                                    pattern=[[-1, P]], channel_multiplier=1).then_inc(s_id, 1)
            pool.wait_ge(s_id, 2)
            nc.gpsimd.tensor_copy(identb[:], ident[:]).then_inc(s_id, 1)
            for p in range(2):
                nc.gpsimd.memset(v_aug[p][:, :, D:2 * D], 1.0).then_inc(s_id, 1)
            nc.gpsimd.memset(half_c[:], -0.5).then_inc(s_id, 1)
            with nc.allow_non_contiguous_dma(reason="small vectors"):
                for k, v in enumerate((bq, bk, bv)):
                    pool.dma_start(b_col[:, k, :], v.rearrange("(c p) -> p c", p=P)).then_inc(s_small, 16)
                for dst, v in ((bo_row, bo), (fb_row, fb)):
                    pool.dma_start(dst[:], v.rearrange("(o n) -> o n", o=1).to_broadcast([P, E])).then_inc(s_small, 16)
                for k, v in enumerate((g_x, g_f)):
                    pool.dma_start(gates[:, k:k + 1], v.rearrange("(o n) -> o n", o=1).to_broadcast([P, 1])).then_inc(s_small, 16)
                for k, v in enumerate((s_in, s_k)):
                    pool.dma_start(scl[:, k:k + 1], v.rearrange("(o n) -> o n", o=1).to_broadcast([P, 1])).then_inc(s_small, 16)
                pool.dma_start(fk_sb[:], fk.rearrange("(c p) n -> p c n", p=P)).then_inc(s_small, 16)
            pool.wait_ge(s_id, 6)

            def layernorm(b, k, src, dst):
                pool.wait_ge(s_mv[k], b + 1)
                carry(pool)
                nc.gpsimd.tensor_scalar(var[k][:], mv[k][:, :, 1], EPS, None, ALU.add).then_inc(s_ln[k], 1)
                pool.wait_ge(s_ln[k], 4 * b + 1)
                nc.gpsimd.tensor_tensor(rstd[k][:], var[k][:], half_c[:], ALU.pow).then_inc(s_ln[k], 1)
                pool.wait_ge(s_ln[k], 4 * b + 2)
                nc.gpsimd.tensor_tensor(nmr[k][:], mv[k][:, :, 0], rstd[k][:], ALU.mult).then_inc(s_ln[k], 1)
                pool.wait_ge(s_ln[k], 4 * b + 3)
                carry(pool)
                nc.gpsimd.tensor_scalar(nmr[k][:], nmr[k][:], -1.0, None, ALU.mult).then_inc(s_ln[k], 1)
                pool.wait_ge(s_ln[k], 4 * b + 4)
                carry(pool)
                for t in range(TT):
                    ins = nc.gpsimd.tensor_scalar(dst[:, t, :], src[:, t, :], rstd[k][:, t:t + 1], nmr[k][:, t:t + 1],
                                                  ALU.mult, ALU.add)
                ins.then_inc(s_xn[k], 1)

            def front_layernorm(b):
                pool.wait_ge(s_ft, at(b))
                layernorm(b, 0, x_in, xn_sb)

            def split_operands(b):
                for k in range(2):
                    pool.wait_ge((s_qm, s_km)[k], at(QK_MOVES * b))
                    pool.wait_ge(s_pe, at(2 * b + 1 + k))
                    carry(pool)
                    base = 10 * b + 5 * k
                    hi, mid, lo = split[k]
                    nc.gpsimd.tensor_copy(hi[:], proj[k][:]).then_inc(s_sp, 1)
                    pool.wait_ge(s_sp, base + 1)
                    nc.gpsimd.tensor_tensor(rest[:], proj[k][:], hi[:], ALU.subtract).then_inc(s_sp, 1)
                    pool.wait_ge(s_sp, base + 2)
                    carry(pool)
                    nc.gpsimd.tensor_copy(mid[:], rest[:]).then_inc(s_sp, 1)
                    pool.wait_ge(s_sp, base + 3)
                    nc.gpsimd.tensor_tensor(rest[:], rest[:], mid[:], ALU.subtract).then_inc(s_sp, 1)
                    pool.wait_ge(s_sp, base + 4)
                    carry(pool)
                    nc.gpsimd.tensor_copy(lo[:], rest[:]).then_inc(s_sp, 1)
                    pool.wait_ge(s_sp, base + 5)

            def queries_by_head(b, p):
                pool.wait_ge(s_qm, QK_MOVES * (b + 1))
                pool.wait_ge(s_S, at(16 * (b - 1)))
                carry(pool)
                nc.gpsimd.tensor_copy(qs[p][:].rearrange("d h j t -> d j h t"),
                                      q_rows[:].rearrange("d j (h t) -> d j h t", t=D)).then_inc(s_qh, 1)

            def values_by_head(b, half):
                pool.wait_ge(s_v, V_MOVES * (2 * b + half + 1))
                pool.wait_ge(s_vt, at(2 * b + half))
                carry(pool)
                nc.gpsimd.tensor_copy(vh[:].rearrange("d h t j -> d j h t"),
                                      vt[:].rearrange("d j (h t) -> d j h t", t=D)).then_inc(s_vh, 1)

            def normalise_attention(b, p):
                pool.wait_ge(s_xr, 16 * (b + 1))
                for t in range(TT):
                    ins = nc.gpsimd.tensor_tensor(x_res[p][:, t, :], x_res[p][:, t, :], bo_row[:], ALU.add)
                ins.then_inc(s_xg, 1)
                pool.wait_ge(s_rec, b + 1)
                pool.wait_ge(s_Om, O_MOVES * (b + 1))
                nc.gpsimd.tensor_tensor(attT[:], attT[:], recT[:], ALU.mult).then_inc(s_norm, 1)

            def quantise(b, p):
                pool.wait_ge(s_y, at(b))
                carry(pool)
                layernorm(b, 1, x_res[p], xb_sb)
                pool.wait_ge(s_mg, b + 1)
                nc.gpsimd.tensor_tensor(ysum_sb[:], y_sb[:], magic_sb[:], ALU.add).then_inc(s_add, 1)
                pool.wait_ge(s_add, b + 1)
                pool.wait_ge(s_qt, at(b))
                nc.gpsimd.tensor_tensor(xq_sb[:], ysum_sb[:], magic_sb[:], ALU.subtract).then_inc(s_q, 1)

            pool.wait_ge(s_init, 3)
            front_layernorm(0)
            split_operands(0)
            queries_by_head(0, 0)
            values_by_head(0, 0)
            values_by_head(0, 1)
            front_layernorm(1)
            split_operands(1)
            queries_by_head(1, 1)
            front_layernorm(2)

            def batch(b, p, prev, one_more, two_more, three_more):
                if prev:
                    normalise_attention(b - 1, 1 - p)
                if one_more:
                    values_by_head(b + 1, 0)
                if two_more:
                    split_operands(b + 2)
                if prev:
                    quantise(b - 1, 1 - p)
                if one_more:
                    values_by_head(b + 1, 1)
                if two_more:
                    queries_by_head(b + 2, p)
                if three_more:
                    front_layernorm(b + 3)

            schedule(pool, batch)
            normalise_attention(NB - 1, 1)
            quantise(NB - 1, 1)

        @block.tensor
        def _(pe):
            pe.wait_ge(s_id, 6)
            for k in range(4):
                pe.wait_ge(s_w, 16 * (k + 1))
                pe.wait_ge(s_wev, at(k))
                for ic in range(EC):
                    for oc in range(EC):
                        ins = nc.tensor.transpose(ps_a[:, ic * E + oc * P:ic * E + oc * P + P],
                                                  w_raw[:, oc, ic * P:ic * P + P], ident[:])
                ins.then_inc(s_wps, 1)
            pe.wait_ge(s_wev, 4)

            def front_transposes(b):
                pe.wait_ge(s_xn[0], b + 1)
                pe.wait_ge(s_ctx, 16 * b + 16)
                pe.wait_ge(s_pv, at(b))
                pe.wait_ge(s_va, at(b if isinstance(b, int) and b == 1 else b - 1))
                for dst, src in ((ps_a, xn_sb), (ps_b, ctx_sb)):
                    for c in range(EC):
                        for t in range(TT):
                            ins = nc.tensor.transpose(dst[:, c * TOK + t * P:c * TOK + t * P + P],
                                                      src[:, t, c * P:c * P + P], ident[:])
                ins.then_inc(s_ft, 1)

            def project(b, k):
                if k == 0:
                    pe.wait_ge(s_fe, 2 * b + 2)
                if k == 2:
                    pe.wait_ge(s_pe, 2 * b + 1)
                dst, src = ((ps_a, xT), (ps_b, cT), (ps_a, cT))[k]
                for oc in range(EC):
                    for ic in range(EC):
                        ins = nc.tensor.matmul(dst[:, oc * TOK:(oc + 1) * TOK], wT[k][:, ic, oc * P:oc * P + P],
                                               src[:, ic, :], start=(ic == 0), stop=(ic == EC - 1))
                ins.then_inc(s_fv if k == 2 else s_fp, 1)

            def value_transposes(b, half, keys_out):
                pe.wait_ge(s_vh, 2 * b + half + 1)
                carry(pe)
                pe.wait_ge(s_pe, at(2 * keys_out))
                carry(pe)
                for hl in range(GH):
                    h = GH * half + hl
                    for kc in range(2):
                        ins = nc.tensor.transpose(ps_b[:, (2 * h + kc) * D:(2 * h + kc + 1) * D],
                                                  vh[:, hl, 8 * kc:8 * kc + 8, :].rearrange("d t j -> d (t j)"),
                                                  ident[0:D, 0:D])
                ins.then_inc(s_vt, 1)

            def scores(b, p, g, n):
                H = 16 * b + GH * g + n
                h = head_of(g, n)
                if g == 0 and n == 0:
                    pe.wait_ge(s_qh, b + 1)
                    pe.wait_ge(s_km, QK_MOVES * (b + 1))
                pe.wait_ge(s_copied, at(H - 1))
                for jh in range(2):
                    ins = nc.tensor.matmul(ps_s[:, n % 2, jh * TOK:(jh + 1) * TOK],
                                           qs[p][:, h, 8 * jh:8 * jh + 8, :].rearrange("d j t -> d (j t)"),
                                           ks[p][:, :, D * h:D * h + D], start=True, stop=True)
                ins.then_inc(s_S, 1)

            def prob_transposes(i, n):
                H = GH * i + n
                pe.wait_ge(s_P, H + 1)
                pe.wait_ge(s_PT, at(H - 1))
                for kc in range(2):
                    for jh in range(2):
                        ins = nc.tensor.transpose(ps_t[:, n % 2, kc * TOK + jh * P:kc * TOK + jh * P + P],
                                                  p_sb[:, n % 2, jh, kc * P:kc * P + P], ident[:])
                ins.then_inc(s_T, 1)

            def mix(b, p, g, n):
                H = 16 * b + GH * g + n
                c, half = n % 4, n // 4
                h = head_of(g, n)
                if g == 0 and n == 0:
                    pe.wait_ge(s_va, b + 1)
                pe.wait_ge(s_PT, H + 1)
                if c == 0:
                    pe.wait_ge(s_O, at(4 * b + 2 * g + half))
                for kc in range(2):
                    ins = nc.tensor.matmul(ps_o[32 * c:32 * c + 32, half * TOK:(half + 1) * TOK],
                                           v_aug[p][:, 2 * h + kc, :], pT_sb[:, n % 2, kc * TOK:(kc + 1) * TOK],
                                           start=(kc == 0), stop=(kc == 1), tile_position=(0, 32 * c))
                ins.then_inc(s_PV, 1)

            def out_project(b):
                pe.wait_ge(s_norm, b + 1)
                pe.wait_ge(s_f, at(b))
                for t in range(TT):
                    for c in range(EC):
                        ins = nc.tensor.matmul(ps_x[:, t * E:(t + 1) * E], attT[:, c, t * P:t * P + P], wT[3][:, c, :],
                                               start=(c == 0), stop=(c == EC - 1))
                ins.then_inc(s_op, 1)

            def ffn_transposes(b):
                pe.wait_ge(s_x1, b + 1)
                pe.wait_ge(s_q, b + 1)
                for c in range(EC):
                    for t in range(TT):
                        ins = nc.tensor.transpose(ps_xb[:, c * TOK + t * P:c * TOK + t * P + P],
                                                  xq_sb[:, t, c * P:c * P + P], identb[:])
                ins.then_inc(s_qt, 1)

            def ffn_matmul(b):
                pe.wait_ge(s_qe, b + 1)
                pe.wait_ge(s_kq, 1)
                for t in range(TT):
                    for c in range(EC):
                        ins = nc.tensor.matmul(ps_x[:, t * E:(t + 1) * E], xqT[:, c, t * P:t * P + P], kq_sb[:, c, :],
                                               start=(c == 0), stop=(c == EC - 1))
                ins.then_inc(s_fm, 1)

            for b in range(2):
                front_transposes(b)
                project(b, 0)
                project(b, 1)
                if b == 0:
                    project(b, 2)
                    value_transposes(0, 0, 1)
                    value_transposes(0, 1, 1)
            for g in range(2):
                for n in range(GH):
                    scores(0, 0, g, n)

            def batch(b, p, prev, one_more, two_more, three_more):
                for g in range(2):
                    for n in range(GH):
                        if one_more:
                            scores(b + 1, 1 - p, g, n)
                        prob_transposes(2 * b + g, n)
                        if n:
                            mix(b, p, g, n - 1)
                        if one_more and (g, n) == (0, 0):
                            project(b + 1, 2)
                        if two_more and (g, n) == (0, 2):
                            front_transposes(b + 2)
                        if two_more and (g, n) == (0, 4):
                            project(b + 2, 0)
                            project(b + 2, 1)
                        if prev and (g, n) == (0, 5):
                            out_project(b - 1)
                        if prev and (g, n) == (1, 2):
                            ffn_transposes(b - 1)
                        if one_more and (g, n) == (1, 3):
                            value_transposes(b + 1, 0, b + 3 if two_more else NB)
                        if prev and (g, n) == (1, 4):
                            ffn_matmul(b - 1)
                    mix(b, p, g, GH - 1)
                if one_more:
                    value_transposes(b + 1, 1, b + 3 if two_more else NB)

            schedule(pe, batch)
            out_project(NB - 1)
            ffn_transposes(NB - 1)
            ffn_matmul(NB - 1)

        @block.scalar
        def _(act):
            act.wait_ge(s_small, 16 * 10)
            nc.scalar.activation(tg[:], gates[:], ACT.Tanh).then_inc(s_tanh, 1)
            for k in range(4):
                act.wait_ge(s_wps, k + 1)
                nc.scalar.copy(wT[k][:].rearrange("p c e -> p (c e)"), ps_a[:]).then_inc(s_wev, 1)

            def evacuate_front(b):
                act.wait_ge(s_ft, b + 1)
                act.wait_ge(s_fp, at(2 * b))
                act.wait_ge(s_fv, at(b))
                nc.scalar.copy(xT[:].rearrange("p c t -> p (c t)"), ps_a[:]).then_inc(s_fe, 1)
                nc.scalar.copy(cT[:].rearrange("p c t -> p (c t)"), ps_b[:]).then_inc(s_fe, 1)

            def evacuate_projection(b, k):
                if k < 2:
                    act.wait_ge(s_fp, 2 * b + k + 1)
                    act.wait_ge(s_sp, at(10 * (b - 1) + 5 + 5 * k))
                else:
                    act.wait_ge(s_fv, b + 1)
                    act.wait_ge(s_v, at(V_MOVES * 2 * b))
                src = (ps_a, ps_b, ps_a)[k]
                for c in range(EC):
                    ins = nc.scalar.activation(proj[k][:, c, :], src[:, c * TOK:(c + 1) * TOK], ACT.Identity,
                                               bias=b_col[:, k, c:c + 1], scale=(D ** -0.5 if k == 0 else 1.0))
                ins.then_inc(s_pv if k == 2 else s_pe, 1)

            def evacuate_values(b, p):
                act.wait_ge(s_vt, 2 * b + 2)
                act.wait_ge(s_PV, at(16 * (b - 1)))
                nc.scalar.copy(v_aug[p][:, :, 0:D], ps_b[:].rearrange("p (h d) -> p h d", d=D)).then_inc(s_va, 1)

            def exps(i, slot, n):
                H = GH * i + n
                act.wait_ge(s_sel, 2 * H + 2)
                act.wait_ge(s_P, at(H - 1))
                for jh in range(2):
                    t = 2 * n + jh
                    ins = nc.scalar.activation(e_sb[:, n % 2, jh, :], score_sb[:, slot, t, :], ACT.Exp,
                                               bias=nmx[:, slot, t:t + 1])
                ins.then_inc(s_exp, 1)

            def evacuate_probs(i, n):
                H = GH * i + n
                act.wait_ge(s_T, H + 1)
                act.wait_ge(s_PV, at(H - 1))
                nc.scalar.copy(pT_sb[:, n % 2, :], ps_t[:, n % 2, :]).then_inc(s_PT, 1)

            def evacuate_mixed(b, p, g, half):
                if g == 0 and half == 0:
                    act.wait_ge(s_Om, at(O_MOVES * b))
                act.wait_ge(s_PV, 16 * b + 8 * g + 4 * half + 4)
                q = 2 * g + half
                nc.scalar.copy(o_sb[:, :, D * q:D * q + D],
                               ps_o[:, half * TOK:(half + 1) * TOK].rearrange("p (j t) -> p j t", t=D)).then_inc(s_O, 1)

            def evacuate_quantised(b):
                act.wait_ge(s_qt, b + 1)
                act.wait_ge(s_fm, at(b))
                nc.scalar.copy(xqT[:].rearrange("p c t -> p (c t)"), ps_xb).then_inc(s_qe, 1)

            def evacuate_ffn(b):
                act.wait_ge(s_fm, b + 1)
                act.wait_ge(s_fb, at(b))
                nc.scalar.activation(f_sb[:].rearrange("p t e -> p (t e)"), ps_x[:], ACT.Copy, scale=oscl[:]).then_inc(s_f, 1)

            act.wait_ge(s_init, 3)
            act.wait_ge(s_id, 6)
            for b in range(2):
                evacuate_front(b)
                evacuate_projection(b, 0)
                evacuate_projection(b, 1)
                if b == 0:
                    evacuate_projection(b, 2)
                    evacuate_values(0, 0)

            def batch(b, p, prev, one_more, two_more, three_more):
                for g in range(2):
                    i = 2 * b + g
                    for n in range(GH):
                        exps(i, 2 * p + g, n)
                        if n:
                            evacuate_probs(i, n - 1)
                        if n == 5:
                            evacuate_mixed(b, p, g, 0)
                        if one_more and (g, n) == (0, 1):
                            evacuate_projection(b + 1, 2)
                        if two_more and (g, n) == (0, 3):
                            evacuate_front(b + 2)
                        if two_more and (g, n) == (0, 5):
                            evacuate_projection(b + 2, 0)
                            evacuate_projection(b + 2, 1)
                        if prev and (g, n) == (1, 3):
                            evacuate_quantised(b - 1)
                        if prev and (g, n) == (1, 5):
                            evacuate_ffn(b - 1)
                    evacuate_probs(i, GH - 1)
                    evacuate_mixed(b, p, g, 1)
                if one_more:
                    evacuate_values(b + 1, 1 - p)

            schedule(act, batch)
            evacuate_quantised(NB - 1)
            evacuate_ffn(NB - 1)

        @block.vector
        def _(dve):
            dve.wait_ge(s_small, 16 * 10)
            nc.vector.tensor_scalar(b_col[:, 0, :], b_col[:, 0, :], D ** -0.5, None, ALU.mult).then_inc(s_init, 1)
            nc.vector.tensor_tensor(oscl[:], scl[:, 0:1], scl[:, 1:2], ALU.mult).then_inc(s_init, 1)
            dve.wait_ge(s_tanh, 1)
            nc.vector.tensor_scalar(bo_row[:], bo_row[:], tg[:, 0:1], None, ALU.mult).then_inc(s_init, 1)
            nc.vector.reciprocal(rscl[:], scl[:]).then_inc(s_init, 1)
            dve.wait_ge(s_init, 4)

            def exponent(dst, src):
                return nc.vector.tensor_scalar(dst.bitcast(I32), src.bitcast(I32), 0x7F800000, None, ALU.bitwise_and)

            def magnitude(dst, src):
                return nc.vector.tensor_scalar(dst.bitcast(I32), src.bitcast(I32), 0x7FFFFFFF, None, ALU.bitwise_and)

            def magic(dst):
                return nc.vector.tensor_scalar(dst, dst, 2.0 ** -6, 1.5 * 2.0 ** 20, ALU.max, ALU.mult)

            def link(ins, value):
                ins.then_inc(s_init, 1)
                dve.wait_ge(s_init, at(value))

            link(nc.vector.tensor_scalar(y_sb[:], fk_sb[:], rscl[:, 1:2], None, ALU.mult), 5)
            link(exponent(magic_sb[:], y_sb[:]), 6)
            link(magic(magic_sb[:]), 7)
            link(nc.vector.tensor_tensor(ysum_sb[:], y_sb[:], magic_sb[:], ALU.add), 8)
            link(nc.vector.tensor_tensor(y_sb[:], ysum_sb[:], magic_sb[:], ALU.subtract), 9)
            link(magnitude(yabs_sb[:], y_sb[:]), 10)
            link(nc.vector.tensor_scalar(ysum_sb[:], yabs_sb[:], 448.0, 3.0e38, ALU.is_gt, ALU.mult), 11)
            link(nc.vector.tensor_scalar(ysum_sb[:], ysum_sb[:], 3.0e38, None, ALU.mult), 12)
            link(nc.vector.tensor_tensor(magic_sb[:], ysum_sb[:], ysum_sb[:], ALU.subtract), 13)
            nc.vector.tensor_tensor(kq_sb[:], y_sb[:], magic_sb[:], ALU.add).then_inc(s_kq, 1)
            dve.wait_ge(s_kq, 1)

            def moments(b, k, src):
                dve.wait_ge(s_xn[k], at(b))
                for t in range(TT):
                    nc.vector.bn_stats(stat6[k][:, t, :], src[:, t, :]).then_inc(s_bn[k], 1)
                dve.wait_ge(s_bn[k], at(TT * b + TT))
                carry(dve)
                for t in range(TT):
                    ins = nc.vector.bn_aggr(mv[k][:, t, :], stat6[k][:, t, :])
                ins.then_inc(s_mv[k], 1)

            def front_moments(b):
                dve.wait_ge(s_x, 16 * (b + 1))
                moments(b, 0, x_in)

            def copy_scores(i, slot, n):
                H = GH * i + n
                dve.wait_ge(s_S, H + 1)
                for jh in range(2):
                    t = 2 * n + jh
                    src = ps_s[:, n % 2, jh * TOK:(jh + 1) * TOK].rearrange("p (j t) -> p t j", t=D)
                    dst = score_sb[:, slot, t, :].rearrange("p (t j) -> p t j", j=NJ)
                    ins = nc.vector.tensor_scalar(dst, src, 0.0, None, ALU.add, ALU.max, accum_out=mx[:, slot, t:t + 1])
                ins.then_inc(s_copied, 1)

            def negate_max(i, slot):
                dve.wait_ge(s_copied, at(GH * i + GH))
                nc.vector.tensor_scalar(nmx[:, slot, :], mx[:, slot, :], -1.0, None, ALU.mult).then_inc(s_nm, 1)
                nc.vector.memset(thr[:, slot, :], -BIG / 2).then_inc(s_nm, 1)

            def select(i, slot):
                dve.wait_ge(s_nm, 2 * i + 2)
                carry(dve)
                with dve.Fori(0, GT) as t:
                    T = GT * i + t
                    s = score_sb[:, slot, bass.ds(t, 1), :].rearrange("p o k -> p (o k)")
                    rest_of = work[:, 0, :]
                    nc.vector.tensor_copy(rest_of, s).then_inc(s_step, 1)
                    for r in range(ROUNDS):
                        dve.wait_ge(s_step, 2 * r + 1)
                        nc.vector.max(max8[:], rest_of).then_inc(s_step, 1)
                        dve.wait_ge(s_step, 2 * r + 2)
                        nc.vector.match_replace(rest_of, max8[:], rest_of, -BIG).then_inc(s_step, 1)
                    dve.wait_ge(s_step, 2 * ROUNDS + 1)
                    nc.vector.tensor_scalar(work[:, 1, :], work[:, 0, :], -BIG / 2, -BIG, ALU.is_gt, ALU.mult).then_inc(s_step, 1)
                    dve.wait_ge(s_step, 2 * ROUNDS + 2)
                    dve.sem_clear(s_step)
                    nc.vector.tensor_tensor(s, s, work[:, 1, :], ALU.add).then_inc(s_sel, 1)
                    dve.wait_ge(s_sel, T + 1)
                    carry(dve)

            def probs(i, slot, n):
                H = GH * i + n
                dve.wait_ge(s_exp, H + 1)
                dve.wait_ge(s_T, at(H - 1))
                for jh in range(2):
                    t = 2 * n + jh
                    ins = nc.vector.scalar_tensor_tensor(p_sb[:, n % 2, jh, :], score_sb[:, slot, t, :], thr[:, slot, t:t + 1],
                                                         e_sb[:, n % 2, jh, :], ALU.is_ge, ALU.mult)
                ins.then_inc(s_P, 1)

            def invert(b):
                dve.wait_ge(s_Om, O_MOVES * (b + 1))
                dve.wait_ge(s_norm, at(b))
                nc.vector.reciprocal(recT[:], denT[:]).then_inc(s_rec, 1)

            def update_residual(b, p):
                dve.wait_ge(s_op, b + 1)
                dve.wait_ge(s_xg, b + 1)
                for t in range(TT):
                    ins = nc.vector.scalar_tensor_tensor(x_res[p][:, t, :], ps_x[:, t * E:(t + 1) * E], tg[:, 0:1],
                                                         x_res[p][:, t, :], ALU.mult, ALU.add)
                ins.then_inc(s_x1, 1)
                dve.wait_ge(s_x1, b + 1)
                moments(b, 1, x_res[p])

            def prepare_rounding(b):
                dve.wait_ge(s_xn[1], b + 1)
                dve.wait_ge(s_q, at(b))
                nc.vector.tensor_scalar(y_sb[:], xb_sb[:], rscl[:, 0:1], None, ALU.mult).then_inc(s_y, 1)
                dve.wait_ge(s_y, b + 1)
                exponent(magic_sb[:], y_sb[:]).then_inc(s_yb, 1)
                dve.wait_ge(s_yb, b + 1)
                magic(magic_sb[:]).then_inc(s_mg, 1)
                magnitude(yabs_sb[:], y_sb[:]).then_inc(s_nan, 1)
                dve.wait_ge(s_nan, 5 * b + 1)
                nc.vector.tensor_reduce(rowmax[:], yabs_sb[:], AX.X, ALU.max).then_inc(s_nan, 1)
                dve.wait_ge(s_nan, 5 * b + 2)
                nc.vector.tensor_scalar(nanrow[:], rowmax[:], 464.0, 3.0e38, ALU.is_gt, ALU.mult).then_inc(s_nan, 1)
                dve.wait_ge(s_nan, 5 * b + 3)
                nc.vector.tensor_scalar(nanrow[:], nanrow[:], 3.0e38, None, ALU.mult).then_inc(s_nan, 1)
                dve.wait_ge(s_nan, 5 * b + 4)
                nc.vector.tensor_tensor(rowmax[:], nanrow[:], nanrow[:], ALU.subtract).then_inc(s_nan, 1)

            def finish(b, p):
                dve.wait_ge(s_f, b + 1)
                dve.wait_ge(s_nan, 5 * b + 5)
                for t in range(TT):
                    ins = nc.vector.scalar_tensor_tensor(fbias_sb[:, t, :], f_sb[:, t, :], rowmax[:, t:t + 1], fb_row[:],
                                                         ALU.add, ALU.add)
                ins.then_inc(s_fb, 1)
                dve.wait_ge(s_fb, b + 1)
                nc.vector.scalar_tensor_tensor(x_res[p][:], fbias_sb[:], tg[:, 1:2], x_res[p][:],
                                               ALU.mult, ALU.add).then_inc(s_res, 1)

            front_moments(0)
            front_moments(1)
            front_moments(2)
            for i in range(2):
                for n in range(GH):
                    copy_scores(i, i, n)
                negate_max(i, i)

            def batch(b, p, prev, one_more, two_more, three_more):
                for g in range(2):
                    i = 2 * b + g
                    slot = 2 * p + g
                    select(i, slot)
                    for n in range(GH):
                        if one_more:
                            copy_scores(i + 2, (slot + 2) % RING, n)
                        probs(i, slot, n)
                        if prev and (g, n) == (0, 2):
                            invert(b - 1)
                        if prev and (g, n) == (0, 5):
                            update_residual(b - 1, 1 - p)
                        if three_more and (g, n) == (1, 0):
                            front_moments(b + 3)
                        if prev and (g, n) == (1, 1):
                            prepare_rounding(b - 1)
                        if prev and (g, n) == (1, 6):
                            finish(b - 1, 1 - p)
                    if one_more:
                        negate_max(i + 2, (slot + 2) % RING)

            schedule(dve, batch)
            invert(NB - 1)
            update_residual(NB - 1, 1)
            prepare_rounding(NB - 1)
            finish(NB - 1, 1)


INS = ['x', 'ctx_1024', 'g_xattn', 'g_ffn', 'L0_xattn_Wq', 'L0_xattn_bq', 'L0_xattn_Wk', 'L0_xattn_bk', 'L0_xattn_Wv',
       'L0_xattn_bv', 'L0_xattn_Wo', 'L0_xattn_bo', 'L0_ffn_kernel', 'L0_ffn_input_scale', 'L0_ffn_kernel_scale',
       'L0_ffn_bias']


def kernel(**inputs):
    import numpy as _np
    import concourse.bacc as _bacc
    from concourse import mybir as _mybir
    from concourse.bass_utils import run_bass_kernel_spmd as _run

    nc = _bacc.Bacc("TRN2", target_bir_lowering=False, num_devices=1)
    arrays, args = {}, []
    for name in INS:
        a = _np.ascontiguousarray(inputs[name])
        arrays[f"in_{name}"] = a
        args.append(nc.dram_tensor(f"in_{name}", a.shape, _mybir.dt.from_np(a.dtype), kind="ExternalInput").ap())
    args.append(nc.dram_tensor("out_0", (NB, TOK, E), F32, kind="ExternalOutput").ap())
    build(nc, *args)
    r = _run(nc, [arrays], core_ids=[0])
    return r.results[0]["out_0"]
```

```python
from contextlib import ExitStack

import concourse.bass as bass
from concourse import mybir

ALU = mybir.AluOpType
ACT = mybir.ActivationFunctionType
AX = mybir.AxisListType
BF16 = mybir.dt.bfloat16
F32 = mybir.dt.float32
I32 = mybir.dt.int32

P = 128
NB = 32
TOK = 256
E = 256
D = 16
NJ = E // D
EC = E // P
TT = TOK // P
NTILE = NB * TT
TOPK = 64
GH = 8
GT = 2 * GH
RING = 4
SPLITS = 96
EPS = 1e-5
BIG = 3.0e38
Q_LEVELS = (0, 0, 1, 1, 0, 2)
K_LEVELS = (0, 1, 0, 1, 2, 0)
ROUNDS = TOPK // 8
GUIDES = 4
ACT_TILES = 12
AIM = 60.0
START = 0.25
SLOPE = 0.0044 / 2
QUARTER = GT // GUIDES


def at(count):
    return max(count, 0) if isinstance(count, int) else count


def head_of(g, n):
    return 4 * (n % 4) + 2 * g + n // 4


def build(nc, x, ctx_in, g_x, g_f, Wq, bq, Wk, bk, Wv, bv, Wo, bo, fk, s_in, s_k, fb, out):
    with ExitStack() as stack:
        def sb(name, shape, dt=F32):
            return stack.enter_context(nc.sbuf_tensor(name, shape, dt))

        def ps(name, shape, dt=F32):
            return stack.enter_context(nc.psum_tensor(name, shape, dt))

        def sem(name):
            return stack.enter_context(nc.semaphore(name))

        x_in = sb("x_in", [P, TT, E])
        ctx_sb = sb("ctx_sb", [P, TT, E])
        xn_sb = sb("xn_sb", [P, TT, E])
        xT = sb("xT", [P, EC, TOK])
        cT = sb("cT", [P, EC, TOK])
        proj = [sb(f"proj{k}", [P, EC, TOK]) for k in range(3)]
        split = [sb(f"split{k}", [P, 3, EC, TOK], BF16) for k in range(2)]
        rest = sb("rest", [P, EC, TOK])
        q_rows = sb("q_rows", [SPLITS, NJ, TOK], BF16)
        qs = [sb(f"qs{p}", [SPLITS, NJ, NJ, D], BF16) for p in range(2)]
        ks = [sb(f"ks{p}", [SPLITS, NJ, TOK], BF16) for p in range(2)]
        v_aug = [sb(f"v_aug{p}", [P, 2 * NJ, 2 * D]) for p in range(2)]
        score_sb = sb("score_sb", [P, RING, GT, TOK])
        mx = sb("mx", [P, RING, GT])
        nmx = sb("nmx", [P, RING, GT])
        thr = sb("thr", [P, RING, GT])
        max8 = sb("max8", [P, 8])
        X = [sb(f"X{k}", [P, 2, GT]) for k in range(2)]
        A = sb("A", [P, 2, GT])
        B = sb("B", [P, 2, GT])
        AB = sb("AB", [P, 2, GT])
        neg_t = sb("neg_t", [P, GT])
        count = sb("count", [P, GT])
        aim = sb("aim", [P, GT])
        newton = sb("newton", [P, GT])
        chord = sb("chord", [P, GT])
        square = sb("square", [P, GT])
        above = sb("above", [P, 2, GT], I32)
        below = sb("below", [P, 2, GT], I32)
        far = sb("far", [P, GT], I32)
        both = sb("both", [P, GT], I32)
        twos = sb("twos", [P, TOK])
        act_junk = sb("act_junk", [P, ACT_TILES, TOK], BF16)
        dve_junk = sb("dve_junk", [P, GT - ACT_TILES, TOK], BF16)
        masked = sb("masked", [P, QUARTER, TOK])
        work = masked[:, 0:2, :]
        final_count = sb("final_count", [P, GT])
        next8 = sb("next8", [P, GT, 8])
        ranks = sb("ranks", [P, 7])
        place = sb("place", [P, GT, 7])
        pick = sb("pick", [P, GT, 7])
        s64 = sb("s64", [P, GT])
        s65 = sb("s65", [P, GT])
        unsure = sb("unsure", [P, GT])
        unsure_b = sb("unsure_b", [P, GT])
        unsure_f = sb("unsure_f", [1, GT + 1])
        unsure_i = sb("unsure_i", [1, GT + 1], I32)
        ones_c = sb("ones_c", [P, 1])
        ones_r = sb("ones_r", [1, P])
        bv_row = sb("bv_row", [1, E])
        e_sb = sb("e_sb", [P, 2, 2, TOK])
        p_sb = sb("p_sb", [P, 2, 2, TOK])
        pT_sb = sb("pT_sb", [P, 2, 2 * TOK])
        o_sb = sb("o_sb", [P, NJ, 4 * D])
        attT = sb("attT", [P, EC, TOK])
        denT = sb("denT", [P, EC, TOK])
        recT = sb("recT", [P, EC, TOK])
        x_res = [sb(f"x_res{p}", [P, TT, E]) for p in range(2)]
        xb_sb = sb("xb_sb", [P, TT, E], BF16)
        y_sb = sb("y_sb", [P, TT, E])
        magic_sb = sb("magic_sb", [P, TT, E])
        ysum_sb = sb("ysum_sb", [P, TT, E])
        yabs_sb = sb("yabs_sb", [P, TT, E])
        xq_sb = sb("xq_sb", [P, TT, E], BF16)
        xqT = sb("xqT", [P, EC, TOK], BF16)
        f_sb = sb("f_sb", [P, TT, E], BF16)
        fbias_sb = sb("fbias_sb", [P, TT, E], BF16)
        w_raw = score_sb[:, RING - 1, 0:EC, :]
        wT = [sb(f"wT{k}", [P, EC, E]) for k in range(4)]
        b_col = sb("b_col", [P, 3, EC])
        bo_row = sb("bo_row", [P, E])
        fb_row = sb("fb_row", [P, E], BF16)
        fk_sb = sb("fk_sb", [P, EC, E], BF16)
        kq_sb = sb("kq_sb", [P, EC, E], BF16)
        gates = sb("gates", [P, 2])
        tg = sb("tg", [P, 2])
        scl = sb("scl", [P, 2])
        rscl = sb("rscl", [P, 2])
        oscl = sb("oscl", [P, 1])
        half_c = sb("half_c", [P, TT])
        ident = sb("ident", [P, P])
        identb = sb("identb", [P, P], BF16)
        stat6 = [sb(f"stat6_{k}", [P, TT, 6]) for k in range(2)]
        mv = [sb(f"mv_{k}", [P, TT, 2]) for k in range(2)]
        var = [sb(f"var_{k}", [P, TT]) for k in range(2)]
        rstd = [sb(f"rstd_{k}", [P, TT]) for k in range(2)]
        nmr = [sb(f"nmr_{k}", [P, TT]) for k in range(2)]
        rowmax = sb("rowmax", [P, TT])
        nanrow = sb("nanrow", [P, TT])

        ps_s = ps("ps_s", [P, 2, 512])
        ps_t = ps("ps_t", [P, 2, 512])
        ps_o = ps("ps_o", [P, 512])
        ps_a = ps("ps_a", [P, 512])
        ps_b = ps("ps_b", [P, 512])
        ps_x = ps("ps_x", [P, 512])
        ps_xb = ps_x[:, 0:TOK].bitcast(BF16)

        s_carrier = sem("register_waits_carried")
        s_w = sem("weights_loaded")
        s_small = sem("small_loaded")
        s_wps = sem("weight_in_psum")
        s_wev = sem("weight_evacuated")
        s_id = sem("constants_ready")
        s_tanh = sem("tanh_done")
        s_init = sem("setup_steps")
        s_kq = sem("kernel_quantised")
        s_x = sem("x_loaded")
        s_ctx = sem("ctx_loaded")
        s_mv = [sem(f"moments_ready{k}") for k in range(2)]
        s_bn = [sem(f"halves_ready{k}") for k in range(2)]
        s_ln = [sem(f"layernorm_steps{k}") for k in range(2)]
        s_xn = [sem(f"normalised{k}") for k in range(2)]
        s_sp = sem("split_steps")
        s_ft = sem("front_transposed")
        s_fe = sem("front_evacuated")
        s_fp = sem("projection_in_psum")
        s_pe = sem("projection_evacuated")
        s_qd = sem("query_levels_in_dram")
        s_kd = sem("key_levels_in_dram")
        s_vd = sem("values_in_dram")
        s_od = sem("mixed_in_dram")
        s_t0 = sem("thresholds_started")
        s_upd = sem("update_steps")
        s_thr = sem("thresholds_moved")
        s_cnt = sem("counted_by_scalar")
        s_dcnt = sem("counted_by_vector")
        s_fin = sem("final_steps")
        s_flag = sem("unsure_rows_known")
        s_fsum = sem("unsure_rows_summed")
        s_load = sem("unsure_counts_ready")
        s_qm = sem("queries_moved")
        s_km = sem("keys_moved")
        s_qh = sem("queries_by_head")
        s_fv = sem("value_projection_in_psum")
        s_pv = sem("value_projection_evacuated")
        s_va = sem("values_ready")
        s_S = sem("scores_in_psum")
        s_copied = sem("scores_copied")
        s_step = sem("selection_steps")
        s_sel = sem("selected")
        s_exp = sem("exp_done")
        s_P = sem("probs_ready")
        s_T = sem("probs_transposed")
        s_PT = sem("probs_evacuated")
        s_PV = sem("values_mixed")
        s_O = sem("mixed_evacuated")
        s_Om = sem("mixed_moved")
        s_rec = sem("denominators_inverted")
        s_norm = sem("attention_normalised")
        s_xr = sem("residual_loaded")
        s_xg = sem("residual_prepared")
        s_op = sem("out_projected")
        s_x1 = sem("residual_updated")
        s_y = sem("scaled")
        s_yb = sem("exponent_taken")
        s_mg = sem("magic_ready")
        s_nan = sem("range_checked")
        s_add = sem("magic_added")
        s_q = sem("quantised")
        s_qt = sem("quantised_transposed")
        s_qe = sem("quantised_evacuated")
        s_fm = sem("ffn_in_psum")
        s_f = sem("ffn_evacuated")
        s_fb = sem("ffn_biased")
        s_res = sem("result_ready")
        s_out = sem("out_stored")

        def carry(eng):
            eng.sem_inc(s_carrier, 1)

        x_dram = x.rearrange("b (t p) e -> b p t e", p=P)
        ctx_dram = ctx_in.rearrange("b (t p) e -> b p t e", p=P)
        out_dram = out.rearrange("b (t p) e -> b p t e", p=P)
        QK_MOVES = len(Q_LEVELS) * 16
        O_MOVES = 2 * EC * 16
        q_scr = nc.dram_tensor("q_scr", (3, E, TOK), BF16).ap()
        k_scr = nc.dram_tensor("k_scr", (3, E, TOK), BF16).ap()
        v_scr = nc.dram_tensor("v_scr", (TOK, E), F32).ap()
        o_scr = nc.dram_tensor("o_scr", (2 * D, NJ, TOK), F32).ap()

        def one(ap, b):
            return ap[bass.ds(b, 1)].rearrange("b p t e -> p (b t) e")

        def schedule(eng, batch):
            for b in range(2):
                batch(b, b, lambda d, b=b: 0 <= b + d < NB)
            with eng.Fori(2, NB - 4, 2) as i:
                batch(i, 0, lambda d: True)
                batch(i + 1, 1, lambda d: True)
            for b in range(NB - 4, NB):
                batch(b, b % 2, lambda d, b=b: 0 <= b + d < NB)

        block = stack.enter_context(nc.Block())

        @block.sync
        def _(sp):
            def load_front(b):
                sp.wait_ge(s_xn[0], at(b))
                carry(sp)
                sp.dma_start(x_in[:], one(x_dram, b)).then_inc(s_x, 16)
                sp.wait_ge(s_ft, at(b))
                carry(sp)
                sp.dma_start(ctx_sb[:], one(ctx_dram, b)).then_inc(s_ctx, 16)

            def move_operands(b, p):
                for k, (scr, dst, levels, stored, moved) in enumerate(((q_scr, q_rows, Q_LEVELS, s_qd, s_qm),
                                                                       (k_scr, ks[p], K_LEVELS, s_kd, s_km))):
                    sp.wait_ge(s_sp, 10 * b + 5 * k + 5)
                    carry(sp)
                    sp.wait_ge(moved, at(QK_MOVES * b))
                    carry(sp)
                    sp.dma_start(scr.rearrange("l (c p) t -> p (l c) t", p=P),
                                 split[k][:].rearrange("p l c t -> p (l c) t")).then_inc(stored, 16)
                    if k == 0:
                        sp.wait_ge(s_qh, at(b))
                    else:
                        sp.wait_ge(s_S, at(16 * (b - 1)))
                    carry(sp)
                    sp.wait_ge(stored, 16 * (b + 1))
                    carry(sp)
                    for s, lev in enumerate(levels):
                        sp.dma_start(dst[D * s:D * s + D], scr[lev].rearrange("(j d) t -> d j t", d=D)).then_inc(moved, 16)

            def move_values(b, p):
                sp.wait_ge(s_pv, b + 1)
                carry(sp)
                sp.wait_ge(s_va, at(16 * b))
                carry(sp)
                sp.dma_start(v_scr.rearrange("(t p) e -> p t e", p=P), proj[2][:]).then_inc(s_vd, 16)
                sp.wait_ge(s_PV, at(16 * (b - 1)))
                carry(sp)
                sp.wait_ge(s_vd, 16 * (b + 1))
                carry(sp)
                with nc.allow_non_contiguous_dma(reason="one key row of a head is 64 bytes"):
                    sp.dma_start(v_aug[p][:, :, 0:D],
                                 v_scr.rearrange("(k q) (j d) -> (q j) k d", q=8, d=D)).then_inc(s_va, 16)

            def move_out(b):
                sp.wait_ge(s_O, 4 * b + 4)
                carry(sp)
                sp.wait_ge(s_Om, at(O_MOVES * b))
                carry(sp)
                for c in range(4):
                    sp.dma_start(o_scr[:, :, 64 * c:64 * c + 64], o_sb[32 * c:32 * c + 32]).then_inc(s_od, 16)
                sp.wait_ge(s_op, at(b))
                carry(sp)
                sp.wait_ge(s_rec, at(b))
                carry(sp)
                sp.wait_ge(s_od, 64 * (b + 1))
                carry(sp)
                for base, dst in ((0, attT), (D, denT)):
                    for c in range(EC):
                        sp.dma_start(dst[:, c, :],
                                     o_scr[base:base + D, 8 * c:8 * c + 8].rearrange("d j t -> j d t")).then_inc(s_Om, 16)

            for k, w in enumerate((Wq, Wk, Wv, Wo)):
                sp.wait_ge(s_wps, at(k))
                sp.dma_start(w_raw, w.rearrange("(c p) i -> p c i", p=P)).then_inc(s_w, 16)
                if k == 0:
                    load_front(0)
            load_front(1)
            move_operands(0, 0)
            move_values(0, 0)
            move_operands(1, 1)
            load_front(2)

            def batch(b, p, has):
                if has(1):
                    move_values(b + 1, 1 - p)
                if has(3):
                    load_front(b + 3)
                if has(2):
                    move_operands(b + 2, p)
                if has(-1):
                    move_out(b - 1)
                if has(-2):
                    sp.wait_ge(s_res, b - 1)
                    carry(sp)
                    sp.dma_start(one(out_dram, b - 2), x_res[p][:]).then_inc(s_out, 16)
                    sp.wait_ge(s_out, 16 * (b - 1))
                    carry(sp)
                sp.dma_start(x_res[p][:], one(x_dram, b)).then_inc(s_xr, 16)

            schedule(sp, batch)
            move_out(NB - 1)
            for b in (NB - 2, NB - 1):
                sp.wait_ge(s_res, b + 1)
                sp.dma_start(one(out_dram, b), x_res[b % 2][:]).then_inc(s_out, 16)
            sp.wait_ge(s_out, 16 * NB)

        @block.gpsimd
        def _(pool):
            nc.gpsimd.memset(ident[:], 0.0).then_inc(s_id, 1)
            pool.wait_ge(s_id, 1)
            nc.gpsimd.affine_select(out=ident[:], in_=ident[:], compare_op=ALU.not_equal, fill=1.0, base=0,
                                    pattern=[[-1, P]], channel_multiplier=1).then_inc(s_id, 1)
            pool.wait_ge(s_id, 2)
            nc.gpsimd.tensor_copy(identb[:], ident[:]).then_inc(s_id, 1)
            for p in range(2):
                nc.gpsimd.memset(v_aug[p][:, :, D:2 * D], 1.0).then_inc(s_id, 1)
            nc.gpsimd.memset(half_c[:], -0.5).then_inc(s_id, 1)
            nc.gpsimd.memset(twos[:], 2.0).then_inc(s_id, 1)
            nc.gpsimd.memset(ones_c[:], 1.0).then_inc(s_id, 1)
            nc.gpsimd.memset(ones_r[:], 1.0).then_inc(s_id, 1)
            nc.gpsimd.memset(aim[:, 0:ACT_TILES], 2 * AIM - TOK).then_inc(s_id, 1)
            nc.gpsimd.memset(aim[:, ACT_TILES:GT], 2 * AIM).then_inc(s_id, 1)
            for r in range(7):
                nc.gpsimd.memset(ranks[:, r:r + 1], float(TOPK - 1 - r)).then_inc(s_id, 1)
            with nc.allow_non_contiguous_dma(reason="small vectors"):
                for k, v in enumerate((bq, bk, bv)):
                    pool.dma_start(b_col[:, k, :], v.rearrange("(c p) -> p c", p=P)).then_inc(s_small, 16)
                pool.dma_start(bv_row[:], bv.rearrange("(o n) -> o n", o=1)).then_inc(s_small, 16)
                for dst, v in ((bo_row, bo), (fb_row, fb)):
                    pool.dma_start(dst[:], v.rearrange("(o n) -> o n", o=1).to_broadcast([P, E])).then_inc(s_small, 16)
                for k, v in enumerate((g_x, g_f)):
                    pool.dma_start(gates[:, k:k + 1], v.rearrange("(o n) -> o n", o=1).to_broadcast([P, 1])).then_inc(s_small, 16)
                for k, v in enumerate((s_in, s_k)):
                    pool.dma_start(scl[:, k:k + 1], v.rearrange("(o n) -> o n", o=1).to_broadcast([P, 1])).then_inc(s_small, 16)
                pool.dma_start(fk_sb[:], fk.rearrange("(c p) n -> p c n", p=P)).then_inc(s_small, 16)
            pool.wait_ge(s_id, 18)

            def layernorm(b, k, src, dst):
                pool.wait_ge(s_mv[k], b + 1)
                carry(pool)
                nc.gpsimd.tensor_scalar(var[k][:], mv[k][:, :, 1], EPS, None, ALU.add).then_inc(s_ln[k], 1)
                pool.wait_ge(s_ln[k], 4 * b + 1)
                nc.gpsimd.tensor_tensor(rstd[k][:], var[k][:], half_c[:], ALU.pow).then_inc(s_ln[k], 1)
                pool.wait_ge(s_ln[k], 4 * b + 2)
                nc.gpsimd.tensor_tensor(nmr[k][:], mv[k][:, :, 0], rstd[k][:], ALU.mult).then_inc(s_ln[k], 1)
                pool.wait_ge(s_ln[k], 4 * b + 3)
                carry(pool)
                nc.gpsimd.tensor_scalar(nmr[k][:], nmr[k][:], -1.0, None, ALU.mult).then_inc(s_ln[k], 1)
                pool.wait_ge(s_ln[k], 4 * b + 4)
                carry(pool)
                for t in range(TT):
                    ins = nc.gpsimd.tensor_scalar(dst[:, t, :], src[:, t, :], rstd[k][:, t:t + 1], nmr[k][:, t:t + 1],
                                                  ALU.mult, ALU.add)
                ins.then_inc(s_xn[k], 1)

            def front_layernorm(b):
                pool.wait_ge(s_ft, at(b))
                layernorm(b, 0, x_in, xn_sb)

            def split_operands(b):
                for k in range(2):
                    pool.wait_ge((s_qm, s_km)[k], at(QK_MOVES * b))
                    pool.wait_ge(s_pe, at(2 * b + 1 + k))
                    carry(pool)
                    base = 10 * b + 5 * k
                    hi, mid, lo = (split[k][:, lev] for lev in range(3))
                    nc.gpsimd.tensor_copy(hi, proj[k][:]).then_inc(s_sp, 1)
                    pool.wait_ge(s_sp, base + 1)
                    nc.gpsimd.tensor_tensor(rest[:], proj[k][:], hi, ALU.subtract).then_inc(s_sp, 1)
                    pool.wait_ge(s_sp, base + 2)
                    carry(pool)
                    nc.gpsimd.tensor_copy(mid, rest[:]).then_inc(s_sp, 1)
                    pool.wait_ge(s_sp, base + 3)
                    nc.gpsimd.tensor_tensor(rest[:], rest[:], mid, ALU.subtract).then_inc(s_sp, 1)
                    pool.wait_ge(s_sp, base + 4)
                    carry(pool)
                    nc.gpsimd.tensor_copy(lo, rest[:]).then_inc(s_sp, 1)
                    pool.wait_ge(s_sp, base + 5)

            def queries_by_head(b, p):
                pool.wait_ge(s_qm, QK_MOVES * (b + 1))
                pool.wait_ge(s_S, at(16 * (b - 1)))
                carry(pool)
                nc.gpsimd.tensor_copy(qs[p][:].rearrange("d h j t -> d j h t"),
                                      q_rows[:].rearrange("d j (h t) -> d j h t", t=D)).then_inc(s_qh, 1)

            def normalise_attention(b, p):
                pool.wait_ge(s_xr, 16 * (b + 1))
                for t in range(TT):
                    ins = nc.gpsimd.tensor_tensor(x_res[p][:, t, :], x_res[p][:, t, :], bo_row[:], ALU.add)
                ins.then_inc(s_xg, 1)
                pool.wait_ge(s_rec, b + 1)
                pool.wait_ge(s_Om, O_MOVES * (b + 1))
                nc.gpsimd.tensor_tensor(attT[:], attT[:], recT[:], ALU.mult).then_inc(s_norm, 1)

            def second_layernorm(b, p):
                pool.wait_ge(s_y, at(b))
                carry(pool)
                layernorm(b, 1, x_res[p], xb_sb)

            def round_tokens(b):
                pool.wait_ge(s_mg, b + 1)
                nc.gpsimd.tensor_tensor(ysum_sb[:], y_sb[:], magic_sb[:], ALU.add).then_inc(s_add, 1)
                pool.wait_ge(s_add, b + 1)
                pool.wait_ge(s_qt, at(b))
                nc.gpsimd.tensor_tensor(xq_sb[:], ysum_sb[:], magic_sb[:], ALU.subtract).then_inc(s_q, 1)

            pool.wait_ge(s_init, 3)
            front_layernorm(0)
            split_operands(0)
            queries_by_head(0, 0)
            front_layernorm(1)
            split_operands(1)
            queries_by_head(1, 1)
            front_layernorm(2)

            def batch(b, p, has):
                if has(-2):
                    round_tokens(b - 2)
                if has(2):
                    split_operands(b + 2)
                    queries_by_head(b + 2, p)
                if has(3):
                    front_layernorm(b + 3)
                if has(-1):
                    normalise_attention(b - 1, 1 - p)
                    second_layernorm(b - 1, 1 - p)

            schedule(pool, batch)
            round_tokens(NB - 2)
            normalise_attention(NB - 1, 1)
            second_layernorm(NB - 1, 1)
            round_tokens(NB - 1)

        @block.tensor
        def _(pe):
            pe.wait_ge(s_id, 18)
            for k in range(4):
                pe.wait_ge(s_w, 16 * (k + 1))
                pe.wait_ge(s_wev, at(k))
                for ic in range(EC):
                    for oc in range(EC):
                        ins = nc.tensor.transpose(ps_a[:, ic * E + oc * P:ic * E + oc * P + P],
                                                  w_raw[:, oc, ic * P:ic * P + P], ident[:])
                ins.then_inc(s_wps, 1)
            pe.wait_ge(s_wev, 4)

            def front_transposes(b):
                pe.wait_ge(s_xn[0], b + 1)
                pe.wait_ge(s_ctx, 16 * b + 16)
                pe.wait_ge(s_pv, at(b))
                pe.wait_ge(s_pe, at(2 * b))
                for dst, src in ((ps_a, xn_sb), (ps_b, ctx_sb)):
                    for c in range(EC):
                        for t in range(TT):
                            ins = nc.tensor.transpose(dst[:, c * TOK + t * P:c * TOK + t * P + P],
                                                      src[:, t, c * P:c * P + P], ident[:])
                ins.then_inc(s_ft, 1)

            def project(b, k):
                if k == 0:
                    pe.wait_ge(s_fe, 2 * b + 2)
                dst, src = ((ps_a, xT), (ps_b, cT))[k]
                for oc in range(EC):
                    for ic in range(EC):
                        ins = nc.tensor.matmul(dst[:, oc * TOK:(oc + 1) * TOK], wT[k][:, ic, oc * P:oc * P + P],
                                               src[:, ic, :], start=(ic == 0), stop=(ic == EC - 1))
                ins.then_inc(s_fp, 1)

            def project_values(b):
                pe.wait_ge(s_pe, 2 * b + 1)
                for t in range(TT):
                    for ic in range(EC):
                        nc.tensor.matmul(ps_a[:, t * E:(t + 1) * E], cT[:, ic, t * P:(t + 1) * P], wT[2][:, ic, :],
                                         start=(ic == 0), stop=False)
                    ins = nc.tensor.matmul(ps_a[:, t * E:(t + 1) * E], ones_r[:], bv_row[:], start=False, stop=True)
                ins.then_inc(s_fv, 1)

            def scores(b, p, g, n):
                H = 16 * b + GH * g + n
                h = head_of(g, n)
                if g == 0 and n == 0:
                    pe.wait_ge(s_qh, b + 1)
                    pe.wait_ge(s_km, QK_MOVES * (b + 1))
                pe.wait_ge(s_copied, at(H - 1))
                for jh in range(2):
                    ins = nc.tensor.matmul(ps_s[:, n % 2, jh * TOK:(jh + 1) * TOK],
                                           qs[p][:, h, 8 * jh:8 * jh + 8, :].rearrange("d j t -> d (j t)"),
                                           ks[p][:, :, D * h:D * h + D], start=True, stop=True)
                ins.then_inc(s_S, 1)

            def prob_transposes(i, n):
                H = GH * i + n
                pe.wait_ge(s_P, H + 1)
                pe.wait_ge(s_PT, at(H - 1))
                for kc in range(2):
                    for jh in range(2):
                        ins = nc.tensor.transpose(ps_t[:, n % 2, kc * TOK + jh * P:kc * TOK + jh * P + P],
                                                  p_sb[:, n % 2, jh, kc * P:kc * P + P], ident[:])
                ins.then_inc(s_T, 1)

            def mix(b, p, g, n):
                H = 16 * b + GH * g + n
                c, half = n % 4, n // 4
                h = head_of(g, n)
                if g == 0 and n == 0:
                    pe.wait_ge(s_va, 16 * (b + 1))
                pe.wait_ge(s_PT, H + 1)
                if c == 0:
                    pe.wait_ge(s_O, at(4 * b + 2 * g + half))
                for kc in range(2):
                    ins = nc.tensor.matmul(ps_o[32 * c:32 * c + 32, half * TOK:(half + 1) * TOK],
                                           v_aug[p][:, 2 * h + kc, :], pT_sb[:, n % 2, kc * TOK:(kc + 1) * TOK],
                                           start=(kc == 0), stop=(kc == 1), tile_position=(0, 32 * c))
                ins.then_inc(s_PV, 1)

            def out_project(b):
                pe.wait_ge(s_norm, b + 1)
                pe.wait_ge(s_f, at(b))
                for t in range(TT):
                    for c in range(EC):
                        ins = nc.tensor.matmul(ps_x[:, t * E:(t + 1) * E], attT[:, c, t * P:t * P + P], wT[3][:, c, :],
                                               start=(c == 0), stop=(c == EC - 1))
                ins.then_inc(s_op, 1)

            def ffn_transposes(b):
                pe.wait_ge(s_x1, b + 1)
                pe.wait_ge(s_q, b + 1)
                for c in range(EC):
                    for t in range(TT):
                        ins = nc.tensor.transpose(ps_xb[:, c * TOK + t * P:c * TOK + t * P + P],
                                                  xq_sb[:, t, c * P:c * P + P], identb[:])
                ins.then_inc(s_qt, 1)

            def ffn_matmul(b):
                pe.wait_ge(s_qe, b + 1)
                pe.wait_ge(s_kq, 1)
                for t in range(TT):
                    for c in range(EC):
                        ins = nc.tensor.matmul(ps_x[:, t * E:(t + 1) * E], xqT[:, c, t * P:t * P + P], kq_sb[:, c, :],
                                               start=(c == 0), stop=(c == EC - 1))
                ins.then_inc(s_fm, 1)

            def sum_unsure(i):
                pe.wait_ge(s_flag, i + 1)
                pe.wait_ge(s_O, at(2 * i))
                nc.tensor.matmul(ps_o[0:1, 0:GT], ones_c[:], unsure_b[:], start=True, stop=True).then_inc(s_fsum, 1)

            for b in range(2):
                front_transposes(b)
                project(b, 0)
                project(b, 1)
                if b == 0:
                    project_values(0)
            for g in range(2):
                for n in range(GH):
                    scores(0, 0, g, n)

            def mix_stage(b, p, g, n):
                prob_transposes(2 * b + g, n)
                if n:
                    mix(b, p, g, n - 1)

            def batch(b, p, has):
                for g in range(2):
                    mb, mp, mg = (b - 1, 1 - p, 1) if g == 0 else (b, p, 0)
                    mixes = g == 1 or has(-1)
                    if mixes:
                        sum_unsure(2 * mb + mg)
                    for n in range(GH):
                        if has(1):
                            scores(b + 1, 1 - p, g, n)
                        if mixes:
                            mix_stage(mb, mp, mg, n)
                        if has(1) and (g, n) == (0, 0):
                            project_values(b + 1)
                        if has(2) and (g, n) == (0, 1):
                            front_transposes(b + 2)
                        if has(2) and (g, n) == (0, 3):
                            project(b + 2, 0)
                            project(b + 2, 1)
                        if has(-2) and (g, n) == (0, 4):
                            ffn_transposes(b - 2)
                        if has(-2) and (g, n) == (0, 6):
                            ffn_matmul(b - 2)
                        if has(-1) and (g, n) == (1, 4):
                            out_project(b - 1)
                    if mixes:
                        mix(mb, mp, mg, GH - 1)

            schedule(pe, batch)
            sum_unsure(2 * NB - 1)
            for n in range(GH):
                mix_stage(NB - 1, 1, 1, n)
            mix(NB - 1, 1, 1, GH - 1)
            ffn_transposes(NB - 2)
            ffn_matmul(NB - 2)
            out_project(NB - 1)
            ffn_transposes(NB - 1)
            ffn_matmul(NB - 1)

        @block.scalar
        def _(act):
            act.wait_ge(s_small, 16 * 11)
            nc.scalar.activation(tg[:], gates[:], ACT.Tanh).then_inc(s_tanh, 1)
            for k in range(4):
                act.wait_ge(s_wps, k + 1)
                nc.scalar.copy(wT[k][:].rearrange("p c e -> p (c e)"), ps_a[:]).then_inc(s_wev, 1)

            def evacuate_front(b):
                act.wait_ge(s_ft, b + 1)
                act.wait_ge(s_fp, at(2 * b))
                act.wait_ge(s_fv, at(b))
                nc.scalar.copy(xT[:].rearrange("p c t -> p (c t)"), ps_a[:]).then_inc(s_fe, 1)
                nc.scalar.copy(cT[:].rearrange("p c t -> p (c t)"), ps_b[:]).then_inc(s_fe, 1)

            def evacuate_projection(b, k):
                act.wait_ge(s_fp, 2 * b + k + 1)
                act.wait_ge(s_sp, at(10 * (b - 1) + 5 + 5 * k))
                src = (ps_a, ps_b)[k]
                for c in range(EC):
                    ins = nc.scalar.activation(proj[k][:, c, :], src[:, c * TOK:(c + 1) * TOK], ACT.Identity,
                                               bias=b_col[:, k, c:c + 1], scale=(D ** -0.5 if k == 0 else 1.0))
                ins.then_inc(s_pe, 1)

            def evacuate_values(b):
                act.wait_ge(s_fv, b + 1)
                act.wait_ge(s_vd, at(16 * b))
                nc.scalar.copy(proj[2][:].rearrange("p t e -> p (t e)"), ps_a[:]).then_inc(s_pv, 1)

            def guide_counts(i, slot, r):
                act.wait_ge(s_thr, (GUIDES + 1) * i + r + 1)
                for t in range(ACT_TILES):
                    ins = nc.scalar.activation(act_junk[:, t, :], score_sb[:, slot, t, :], ACT.Sign, bias=neg_t[:, t:t + 1],
                                               accum_out=count[:, t:t + 1])
                ins.then_inc(s_cnt, 1)

            def exps(i, slot, n):
                H = GH * i + n
                act.wait_ge(s_sel, i + 1)
                act.wait_ge(s_P, at(H - 1))
                for jh in range(2):
                    t = 2 * n + jh
                    ins = nc.scalar.activation(e_sb[:, n % 2, jh, :], score_sb[:, slot, t, :], ACT.Exp,
                                               bias=nmx[:, slot, t:t + 1])
                ins.then_inc(s_exp, 1)

            def evacuate_probs(i, n):
                H = GH * i + n
                act.wait_ge(s_T, H + 1)
                act.wait_ge(s_PV, at(H - 1))
                nc.scalar.copy(pT_sb[:, n % 2, :], ps_t[:, n % 2, :]).then_inc(s_PT, 1)

            def evacuate_mixed(b, p, g, half):
                if g == 0 and half == 0:
                    act.wait_ge(s_Om, at(O_MOVES * b))
                act.wait_ge(s_PV, 16 * b + 8 * g + 4 * half + 4)
                q = 2 * g + half
                nc.scalar.copy(o_sb[:, :, D * q:D * q + D],
                               ps_o[:, half * TOK:(half + 1) * TOK].rearrange("p (j t) -> p j t", t=D)).then_inc(s_O, 1)

            def evacuate_quantised(b):
                act.wait_ge(s_qt, b + 1)
                act.wait_ge(s_fm, at(b))
                nc.scalar.copy(xqT[:].rearrange("p c t -> p (c t)"), ps_xb).then_inc(s_qe, 1)

            def evacuate_ffn(b):
                act.wait_ge(s_fm, b + 1)
                act.wait_ge(s_fb, at(b))
                nc.scalar.activation(f_sb[:].rearrange("p t e -> p (t e)"), ps_x[:], ACT.Copy, scale=oscl[:]).then_inc(s_f, 1)

            act.wait_ge(s_init, 3)
            act.wait_ge(s_id, 18)
            for b in range(2):
                evacuate_front(b)
                evacuate_projection(b, 0)
                evacuate_projection(b, 1)
                if b == 0:
                    evacuate_values(0)

            def mix_stage(b, p, g, n):
                i = 2 * b + g
                exps(i, 2 * p + g, n)
                if n:
                    evacuate_probs(i, n - 1)
                if n == 5:
                    evacuate_mixed(b, p, g, 0)

            def batch(b, p, has):
                for g in range(2):
                    mb, mp, mg = (b - 1, 1 - p, 1) if g == 0 else (b, p, 0)
                    mixes = g == 1 or has(-1)
                    guided = g == 0 or has(1)
                    for r in range(GUIDES):
                        if guided:
                            guide_counts(2 * b + g + 1, (2 * p + g + 1) % RING, r)
                        for n in (2 * r, 2 * r + 1):
                            if mixes:
                                mix_stage(mb, mp, mg, n)
                            if has(1) and (g, n) == (0, 1):
                                evacuate_values(b + 1)
                            if has(2) and (g, n) == (0, 2):
                                evacuate_front(b + 2)
                            if has(2) and (g, n) == (0, 4):
                                evacuate_projection(b + 2, 0)
                                evacuate_projection(b + 2, 1)
                            if has(-2) and (g, n) == (0, 5):
                                evacuate_quantised(b - 2)
                            if has(-2) and (g, n) == (0, 7):
                                evacuate_ffn(b - 2)
                    if mixes:
                        evacuate_probs(2 * mb + mg, GH - 1)
                        evacuate_mixed(mb, mp, mg, 1)

            for r in range(GUIDES):
                guide_counts(0, 0, r)
            schedule(act, batch)
            for n in range(GH):
                mix_stage(NB - 1, 1, 1, n)
            evacuate_probs(2 * NB - 1, GH - 1)
            evacuate_mixed(NB - 1, 1, 1, 1)
            for b in (NB - 2, NB - 1):
                evacuate_quantised(b)
                evacuate_ffn(b)

        @block.vector
        def _(dve):
            dve.wait_ge(s_small, 16 * 11)
            nc.vector.tensor_scalar(b_col[:, 0, :], b_col[:, 0, :], D ** -0.5, None, ALU.mult).then_inc(s_init, 1)
            nc.vector.tensor_tensor(oscl[:], scl[:, 0:1], scl[:, 1:2], ALU.mult).then_inc(s_init, 1)
            dve.wait_ge(s_tanh, 1)
            nc.vector.tensor_scalar(bo_row[:], bo_row[:], tg[:, 0:1], None, ALU.mult).then_inc(s_init, 1)
            nc.vector.reciprocal(rscl[:], scl[:]).then_inc(s_init, 1)
            dve.wait_ge(s_init, 4)

            def exponent(dst, src):
                return nc.vector.tensor_scalar(dst.bitcast(I32), src.bitcast(I32), 0x7F800000, None, ALU.bitwise_and)

            def magnitude(dst, src):
                return nc.vector.tensor_scalar(dst.bitcast(I32), src.bitcast(I32), 0x7FFFFFFF, None, ALU.bitwise_and)

            def magic(dst):
                return nc.vector.tensor_scalar(dst, dst, 2.0 ** -6, 1.5 * 2.0 ** 20, ALU.max, ALU.mult)

            def link(ins, value):
                ins.then_inc(s_init, 1)
                dve.wait_ge(s_init, at(value))

            link(nc.vector.tensor_scalar(y_sb[:], fk_sb[:], rscl[:, 1:2], None, ALU.mult), 5)
            link(exponent(magic_sb[:], y_sb[:]), 6)
            link(magic(magic_sb[:]), 7)
            link(nc.vector.tensor_tensor(ysum_sb[:], y_sb[:], magic_sb[:], ALU.add), 8)
            link(nc.vector.tensor_tensor(y_sb[:], ysum_sb[:], magic_sb[:], ALU.subtract), 9)
            link(magnitude(yabs_sb[:], y_sb[:]), 10)
            link(nc.vector.tensor_scalar(ysum_sb[:], yabs_sb[:], 448.0, 3.0e38, ALU.is_gt, ALU.mult), 11)
            link(nc.vector.tensor_scalar(ysum_sb[:], ysum_sb[:], 3.0e38, None, ALU.mult), 12)
            link(nc.vector.tensor_tensor(magic_sb[:], ysum_sb[:], ysum_sb[:], ALU.subtract), 13)
            nc.vector.tensor_tensor(kq_sb[:], y_sb[:], magic_sb[:], ALU.add).then_inc(s_kq, 1)
            dve.wait_ge(s_kq, 1)

            def moments(b, k, src):
                dve.wait_ge(s_xn[k], at(b))
                for t in range(TT):
                    nc.vector.bn_stats(stat6[k][:, t, :], src[:, t, :]).then_inc(s_bn[k], 1)
                dve.wait_ge(s_bn[k], at(TT * b + TT))
                carry(dve)
                for t in range(TT):
                    ins = nc.vector.bn_aggr(mv[k][:, t, :], stat6[k][:, t, :])
                ins.then_inc(s_mv[k], 1)

            def front_moments(b):
                dve.wait_ge(s_x, 16 * (b + 1))
                moments(b, 0, x_in)

            def copy_scores(i, slot, n):
                H = GH * i + n
                dve.wait_ge(s_S, H + 1)
                for jh in range(2):
                    t = 2 * n + jh
                    src = ps_s[:, n % 2, jh * TOK:(jh + 1) * TOK].rearrange("p (j t) -> p t j", t=D)
                    dst = score_sb[:, slot, t, :].rearrange("p (t j) -> p t j", j=NJ)
                    ins = nc.vector.tensor_scalar(dst, src, 0.0, None, ALU.add, ALU.max, accum_out=mx[:, slot, t:t + 1])
                ins.then_inc(s_copied, 1)

            def start_thresholds(i, slot):
                x = X[slot % 2]
                dve.wait_ge(s_copied, GH * i + GH)
                carry(dve)
                dve.wait_ge(s_thr, at((GUIDES + 1) * i))
                carry(dve)
                nc.vector.tensor_scalar(nmx[:, slot, :], mx[:, slot, :], -1.0, None, ALU.mult)
                nc.vector.tensor_scalar(x[:, 0, :], mx[:, slot, :], START, None, ALU.mult)
                nc.vector.tensor_scalar(neg_t[:], mx[:, slot, :], -START, None, ALU.mult).then_inc(s_thr, 1)
                nc.vector.memset(A[:], 1000.0)
                nc.vector.memset(B[:], -1000.0).then_inc(s_t0, 1)
                dve.wait_ge(s_t0, i + 1)
                carry(dve)

            def guide_counts(i, slot, r):
                for t in range(ACT_TILES, GT):
                    ins = nc.vector.scalar_tensor_tensor(dve_junk[:, t - ACT_TILES, :], score_sb[:, slot, t, :], X[slot % 2][:, 0, t:t + 1],
                                                         twos[:], ALU.is_gt, ALU.mult, accum_out=count[:, t:t + 1])
                ins.then_inc(s_dcnt, 1)

            def update_thresholds(i, slot, r):
                x = X[slot % 2]
                done = [0]

                def step(ins):
                    done[0] += 1
                    ins.then_inc(s_upd, 1)
                    dve.wait_ge(s_upd, done[0])

                dve.wait_ge(s_cnt, GUIDES * i + r + 1)
                carry(dve)
                dve.wait_ge(s_dcnt, GUIDES * i + r + 1)
                carry(dve)
                step(nc.vector.tensor_tensor(x[:, 1, :], count[:], aim[:], ALU.subtract))
                off = x[:, 1:2, :].to_broadcast([P, 2, GT])
                nc.vector.tensor_scalar(above[:], off, 0.0, None, ALU.is_gt)
                nc.vector.tensor_scalar(below[:], off, 0.0, None, ALU.is_le)
                nc.vector.tensor_tensor(square[:], x[:, 1, :], x[:, 1, :], ALU.mult)
                step(nc.vector.tensor_tensor(newton[:], x[:, 1, :], mx[:, slot, :], ALU.mult))
                nc.vector.copy_predicated(A[:], above[:], x[:])
                nc.vector.copy_predicated(B[:], below[:], x[:])
                nc.vector.tensor_scalar(far[:], square[:], 40.0, None, ALU.is_gt)
                step(nc.vector.tensor_scalar(newton[:], newton[:], SLOPE, None, ALU.mult))
                step(nc.vector.tensor_tensor(newton[:], newton[:], x[:, 0, :], ALU.add))
                if r:
                    step(nc.vector.tensor_tensor(AB[:], B[:], A[:], ALU.subtract))
                    nc.vector.tensor_scalar(both[:], AB[:, 1, :], -1000.0 + TOK, None, ALU.is_gt)
                    step(nc.vector.reciprocal(chord[:], AB[:, 1, :]))
                    step(nc.vector.tensor_tensor(chord[:], chord[:], A[:, 1, :], ALU.mult))
                    step(nc.vector.tensor_tensor(chord[:], chord[:], AB[:, 0, :], ALU.mult))
                    step(nc.vector.tensor_tensor(chord[:], A[:, 0, :], chord[:], ALU.subtract))
                    step(nc.vector.copy_predicated(newton[:], both[:], chord[:]))
                step(nc.vector.copy_predicated(x[:, 0, :], far[:], newton[:]))
                dve.sem_clear(s_upd)
                nc.vector.tensor_scalar(neg_t[:], x[:, 0, :], -1.0, None, ALU.mult).then_inc(s_thr, 1)

            FINAL = 3 * GT + 7

            def final_tiles(i, slot, q):
                tiles = range(q * QUARTER, (q + 1) * QUARTER)
                base = FINAL * i + 3 * QUARTER * q
                dve.wait_ge(s_fin, at(base))
                carry(dve)
                for k, t in enumerate(tiles):
                    nc.vector.tensor_scalar(masked[:, k, :], score_sb[:, slot, t, :], X[slot % 2][:, 0, t:t + 1], None,
                                            ALU.is_gt, ALU.add, accum_out=final_count[:, t:t + 1]).then_inc(s_fin, 1)
                for k, t in enumerate(tiles):
                    dve.wait_ge(s_fin, base + k + 1)
                    nc.vector.scalar_tensor_tensor(masked[:, k, :], masked[:, k, :], -BIG, score_sb[:, slot, t, :],
                                                   ALU.mult, ALU.add).then_inc(s_fin, 1)
                for k, t in enumerate(tiles):
                    dve.wait_ge(s_fin, base + QUARTER + k + 1)
                    carry(dve)
                    nc.vector.max(next8[:, t, :], masked[:, k, :]).then_inc(s_fin, 1)

            def final_thresholds(i, slot):
                base = FINAL * i + 3 * GT
                dve.wait_ge(s_fin, base)
                nc.vector.tensor_tensor(place[:], final_count[:].rearrange("p (t o) -> p t o", o=1).to_broadcast([P, GT, 7]),
                                        ranks[:].rearrange("p (o r) -> p o r", o=1).to_broadcast([P, GT, 7]),
                                        ALU.is_equal).then_inc(s_fin, 1)
                for k, dst in enumerate((s64, s65)):
                    dve.wait_ge(s_fin, base + 1 + 2 * k)
                    nc.vector.tensor_tensor(pick[:], place[:], next8[:, :, k:k + 7], ALU.mult).then_inc(s_fin, 1)
                    dve.wait_ge(s_fin, base + 2 + 2 * k)
                    nc.vector.tensor_reduce(dst[:], pick[:], AX.X, ALU.add).then_inc(s_fin, 1)
                dve.wait_ge(s_fin, base + 5)
                nc.vector.tensor_copy(thr[:, slot, :], s64[:]).then_inc(s_fin, 1)
                dve.wait_ge(s_fin, base + 6)
                nc.vector.tensor_tensor(unsure[:], s64[:], s65[:], ALU.is_le).then_inc(s_fin, 1)
                dve.wait_ge(s_fin, base + 7)
                nc.vector.tensor_copy(unsure_b[:], unsure[:]).then_inc(s_flag, 1)

            def select_tile(slot, t):
                s = score_sb[:, slot, bass.ds(t, 1), :].rearrange("p o k -> p (o k)")
                rest_of = work[:, 0, :]
                nc.vector.tensor_scalar(thr[:, slot, bass.ds(t, 1)], thr[:, slot, bass.ds(t, 1)], 0.0, -BIG / 2,
                                        ALU.mult, ALU.add)
                nc.vector.tensor_copy(rest_of, s).then_inc(s_step, 1)
                for r in range(ROUNDS):
                    dve.wait_ge(s_step, 2 * r + 1)
                    nc.vector.max(max8[:], rest_of).then_inc(s_step, 1)
                    dve.wait_ge(s_step, 2 * r + 2)
                    nc.vector.match_replace(rest_of, max8[:], rest_of, -BIG).then_inc(s_step, 1)
                dve.wait_ge(s_step, 2 * ROUNDS + 1)
                nc.vector.tensor_scalar(work[:, 1, :], work[:, 0, :], -BIG / 2, -BIG, ALU.is_gt, ALU.mult).then_inc(s_step, 1)
                dve.wait_ge(s_step, 2 * ROUNDS + 2)
                nc.vector.tensor_tensor(s, s, work[:, 1, :], ALU.add).then_inc(s_step, 1)
                dve.wait_ge(s_step, 2 * ROUNDS + 3)
                dve.sem_clear(s_step)

            def settle(i, slot):
                dve.wait_ge(s_fsum, i + 1)
                carry(dve)
                nc.vector.tensor_scalar(unsure_f[:, 0:GT], ps_o[0:1, 0:GT], 0.0, None, ALU.add, ALU.add,
                                        accum_out=unsure_f[:, GT:GT + 1]).then_inc(s_load, 1)
                dve.wait_ge(s_load, 2 * i + 1)
                carry(dve)
                nc.vector.tensor_copy(unsure_i[:], unsure_f[:]).then_inc(s_load, 1)
                dve.wait_ge(s_load, 2 * i + 2)
                carry(dve)
                total = dve.value_load(unsure_i[0:1, GT:GT + 1], min_val=0, max_val=GT * P)
                with dve.If(total > 0):
                    with dve.Fori(0, GT) as t:
                        rows = dve.value_load(unsure_i[0:1, bass.ds(t, 1)], min_val=0, max_val=P)
                        with dve.If(rows > 0):
                            select_tile(slot, t)
                dve.sem_inc(s_sel, 1)

            def probs(i, slot, n):
                H = GH * i + n
                dve.wait_ge(s_exp, H + 1)
                dve.wait_ge(s_T, at(H - 1))
                for jh in range(2):
                    t = 2 * n + jh
                    ins = nc.vector.scalar_tensor_tensor(p_sb[:, n % 2, jh, :], score_sb[:, slot, t, :], thr[:, slot, t:t + 1],
                                                         e_sb[:, n % 2, jh, :], ALU.is_ge, ALU.mult)
                ins.then_inc(s_P, 1)

            def invert(b):
                dve.wait_ge(s_Om, O_MOVES * (b + 1))
                dve.wait_ge(s_norm, at(b))
                nc.vector.reciprocal(recT[:], denT[:]).then_inc(s_rec, 1)

            def update_residual(b, p):
                dve.wait_ge(s_op, b + 1)
                dve.wait_ge(s_xg, b + 1)
                for t in range(TT):
                    ins = nc.vector.scalar_tensor_tensor(x_res[p][:, t, :], ps_x[:, t * E:(t + 1) * E], tg[:, 0:1],
                                                         x_res[p][:, t, :], ALU.mult, ALU.add)
                ins.then_inc(s_x1, 1)
                dve.wait_ge(s_x1, b + 1)
                moments(b, 1, x_res[p])

            def prepare_rounding(b):
                dve.wait_ge(s_xn[1], b + 1)
                dve.wait_ge(s_q, at(b))
                nc.vector.tensor_scalar(y_sb[:], xb_sb[:], rscl[:, 0:1], None, ALU.mult).then_inc(s_y, 1)
                dve.wait_ge(s_y, b + 1)
                exponent(magic_sb[:], y_sb[:]).then_inc(s_yb, 1)
                dve.wait_ge(s_yb, b + 1)
                magic(magic_sb[:]).then_inc(s_mg, 1)
                magnitude(yabs_sb[:], y_sb[:]).then_inc(s_nan, 1)
                dve.wait_ge(s_nan, 5 * b + 1)
                nc.vector.tensor_reduce(rowmax[:], yabs_sb[:], AX.X, ALU.max).then_inc(s_nan, 1)
                dve.wait_ge(s_nan, 5 * b + 2)
                nc.vector.tensor_scalar(nanrow[:], rowmax[:], 464.0, 3.0e38, ALU.is_gt, ALU.mult).then_inc(s_nan, 1)
                dve.wait_ge(s_nan, 5 * b + 3)
                nc.vector.tensor_scalar(nanrow[:], nanrow[:], 3.0e38, None, ALU.mult).then_inc(s_nan, 1)
                dve.wait_ge(s_nan, 5 * b + 4)
                nc.vector.tensor_tensor(rowmax[:], nanrow[:], nanrow[:], ALU.subtract).then_inc(s_nan, 1)

            def finish(b, p):
                dve.wait_ge(s_f, b + 1)
                dve.wait_ge(s_nan, 5 * b + 5)
                for t in range(TT):
                    ins = nc.vector.scalar_tensor_tensor(fbias_sb[:, t, :], f_sb[:, t, :], rowmax[:, t:t + 1], fb_row[:],
                                                         ALU.add, ALU.add)
                ins.then_inc(s_fb, 1)
                dve.wait_ge(s_fb, b + 1)
                nc.vector.scalar_tensor_tensor(x_res[p][:], fbias_sb[:], tg[:, 1:2], x_res[p][:],
                                               ALU.mult, ALU.add).then_inc(s_res, 1)

            front_moments(0)
            front_moments(1)
            front_moments(2)
            for i in range(2):
                for n in range(GH):
                    copy_scores(i, i, n)
                if i == 0:
                    start_thresholds(0, 0)
            for r in range(GUIDES):
                guide_counts(0, 0, r)
                update_thresholds(0, 0, r)

            def batch(b, p, has):
                for g in range(2):
                    i = 2 * b + g
                    slot = 2 * p + g
                    ahead = (slot + 1) % RING
                    fresh = (slot + 2) % RING
                    mixed = (slot - 1) % RING
                    mixes = g == 1 or has(-1)
                    guided = g == 0 or has(1)
                    if guided:
                        start_thresholds(i + 1, ahead)
                    if mixes:
                        settle(i - 1, mixed)
                    for r in range(GUIDES):
                        if guided:
                            guide_counts(i + 1, ahead, r)
                        final_tiles(i, slot, r)
                        for n in (2 * r, 2 * r + 1):
                            if n % 2 == 1 and guided:
                                update_thresholds(i + 1, ahead, r)
                            if has(1):
                                copy_scores(i + 2, fresh, n)
                            if mixes:
                                probs(i - 1, mixed, n)
                            if has(-2) and (g, n) == (0, 1):
                                prepare_rounding(b - 2)
                            if has(-2) and (g, n) == (0, 7):
                                finish(b - 2, p)
                            if has(-1) and (g, n) == (1, 3):
                                invert(b - 1)
                            if has(-1) and (g, n) == (1, 6):
                                update_residual(b - 1, 1 - p)
                            if has(3) and (g, n) == (1, 1):
                                front_moments(b + 3)
                    final_thresholds(i, slot)

            schedule(dve, batch)
            settle(2 * NB - 1, RING - 1)
            for n in range(GH):
                probs(2 * NB - 1, RING - 1, n)
            prepare_rounding(NB - 2)
            finish(NB - 2, 0)
            invert(NB - 1)
            update_residual(NB - 1, 1)
            prepare_rounding(NB - 1)
            finish(NB - 1, 1)


INS = ['x', 'ctx_1024', 'g_xattn', 'g_ffn', 'L0_xattn_Wq', 'L0_xattn_bq', 'L0_xattn_Wk', 'L0_xattn_bk', 'L0_xattn_Wv',
       'L0_xattn_bv', 'L0_xattn_Wo', 'L0_xattn_bo', 'L0_ffn_kernel', 'L0_ffn_input_scale', 'L0_ffn_kernel_scale',
       'L0_ffn_bias']


def kernel(**inputs):
    import numpy as _np
    import concourse.bacc as _bacc
    from concourse import mybir as _mybir
    from concourse.bass_utils import run_bass_kernel_spmd as _run

    nc = _bacc.Bacc("TRN2", target_bir_lowering=False, num_devices=1)
    arrays, args = {}, []
    for name in INS:
        a = _np.ascontiguousarray(inputs[name])
        arrays[f"in_{name}"] = a
        args.append(nc.dram_tensor(f"in_{name}", a.shape, _mybir.dt.from_np(a.dtype), kind="ExternalInput").ap())
    args.append(nc.dram_tensor("out_0", (NB, TOK, E), F32, kind="ExternalOutput").ap())
    build(nc, *args)
    r = _run(nc, [arrays], core_ids=[0])
    return r.results[0]["out_0"]
```

```python
from contextlib import ExitStack

import concourse.bass as bass
from concourse import mybir

ALU = mybir.AluOpType
ACT = mybir.ActivationFunctionType
AX = mybir.AxisListType
BF16 = mybir.dt.bfloat16
F32 = mybir.dt.float32
I32 = mybir.dt.int32

P = 128
NB = 32
TOK = 256
E = 256
D = 16
NJ = E // D
EC = E // P
TT = TOK // P
TOPK = 64
GH = 8
GT = 2 * GH
RING = 4
SPLITS = 96
EPS = 1e-5
BIG = 3.0e38
Q_LEVELS = (0, 0, 1, 1, 0, 2)
K_LEVELS = (0, 1, 0, 1, 2, 0)
ROUNDS = TOPK // 8
GUIDES = 4
ACT_TILES = 14
AIM = 60.5
WINDOW = 8
START = 0.25
SLOPE = 0.0040 / 2
NO_POINT = 1000.0
QUARTER = GT // GUIDES
MASK_LAG, MIX_LAG = 2, 4


def at(count):
    return max(count, 0) if isinstance(count, int) else count


def head_of(g, n):
    return 4 * (n % 4) + 2 * g + n // 4


def earlier(b, p, g, n, lag, before):
    if n >= lag:
        return b, p, g, n - lag
    if before:
        return (b, p, 0, n + GH - lag) if g else (b - 1, 1 - p, 1, n + GH - lag)
    return None


def build(nc, x, ctx_in, g_x, g_f, Wq, bq, Wk, bk, Wv, bv, Wo, bo, fk, s_in, s_k, fb, out):
    with ExitStack() as stack:
        def sb(name, shape, dt=F32):
            return stack.enter_context(nc.sbuf_tensor(name, shape, dt))

        def ps(name, shape, dt=F32):
            return stack.enter_context(nc.psum_tensor(name, shape, dt))

        def sem(name):
            return stack.enter_context(nc.semaphore(name))

        x_in = sb("x_in", [P, TT, E])
        ctx_sb = sb("ctx_sb", [P, TT, E])
        xn_sb = sb("xn_sb", [P, TT, E])
        xT = sb("xT", [P, EC, TOK])
        cT = sb("cT", [P, EC, TOK])
        proj = [sb(f"proj{k}", [P, EC, TOK]) for k in range(3)]
        split = [sb(f"split{k}", [P, 3, EC, TOK], BF16) for k in range(2)]
        rest = sb("rest", [P, EC, TOK])
        q_rows = sb("q_rows", [SPLITS, NJ, TOK], BF16)
        qs = [sb(f"qs{p}", [SPLITS, NJ, NJ, D], BF16) for p in range(2)]
        ks = [sb(f"ks{p}", [SPLITS, NJ, TOK], BF16) for p in range(2)]
        v_aug = [sb(f"v_aug{p}", [P, 2 * NJ, 2 * D]) for p in range(2)]
        score_sb = sb("score_sb", [P, RING, GT, TOK])
        mx = sb("mx", [P, RING, GT])
        nmx = sb("nmx", [P, RING, GT])
        thr = sb("thr", [P, RING, GT])
        max8 = sb("max8", [P, 8])
        X = [sb(f"X{k}", [P, 2, GT]) for k in range(2)]
        A = [sb(f"A{k}", [P, 2, GT]) for k in range(2)]
        B = [sb(f"B{k}", [P, 2, GT]) for k in range(2)]
        AB = sb("AB", [P, 2, GT])
        count = [sb(f"count{k}", [P, GT]) for k in range(2)]
        aim = sb("aim", [P, GT])
        newton = sb("newton", [P, GT])
        product = sb("product", [P, GT])
        chord = sb("chord", [P, GT])
        square = sb("square", [P, GT])
        above = sb("above", [P, 2, GT], I32)
        below = sb("below", [P, 2, GT], I32)
        far = sb("far", [P, GT], I32)
        far_f = sb("far_f", [P, GT])
        both = sb("both", [P, GT], I32)
        minus_twos = sb("minus_twos", [P, TOK])
        act_junk = sb("act_junk", [P, ACT_TILES, TOK], BF16)
        dve_junk = sb("dve_junk", [P, GT - ACT_TILES, TOK], BF16)
        masked = sb("masked", [P, QUARTER, TOK])
        work = masked[:, 0:2, :]
        final_count = sb("final_count", [P, GT])
        following = sb("following", [P, GT, 1 + WINDOW])
        ranks = sb("ranks", [P, WINDOW])
        place = sb("place", [P, GT, WINDOW])
        pick = sb("pick", [P, GT, WINDOW])
        pick65 = sb("pick65", [P, GT, WINDOW])
        s64 = sb("s64", [P, GT])
        s65 = sb("s65", [P, GT])
        unsure_b = sb("unsure_b", [P, GT])
        unsure_f = sb("unsure_f", [1, GT + 1])
        unsure_i = sb("unsure_i", [1, 1], I32)
        numbers = sb("numbers", [1, GT])
        marked = sb("marked", [1, GT + 1])
        listed = sb("listed", [1, GT])
        listed_i = sb("listed_i", [1, GT + 1], I32)
        ones_c = sb("ones_c", [P, 1])
        ones_r = sb("ones_r", [1, P])
        bv_row = sb("bv_row", [1, E])
        e_sb = sb("e_sb", [P, 2, 2, TOK])
        p_sb = sb("p_sb", [P, 2, 2, TOK])
        pT_sb = sb("pT_sb", [P, 2, 2 * TOK])
        o_sb = sb("o_sb", [P, NJ, 4 * D])
        attT = sb("attT", [P, EC, TOK])
        den_sb = sb("den_sb", [P, NJ * TOK // P])
        rec_sb = sb("rec_sb", [P, NJ * TOK // P])
        recT = sb("recT", [P, EC, TOK])
        x_res = [sb(f"x_res{p}", [P, TT, E]) for p in range(2)]
        xb_sb = sb("xb_sb", [P, TT, E], BF16)
        y_sb = sb("y_sb", [P, TT, E])
        magic_sb = sb("magic_sb", [P, TT, E])
        ysum_sb = sb("ysum_sb", [P, TT, E])
        yabs_sb = sb("yabs_sb", [P, TT, E])
        xq_sb = sb("xq_sb", [P, TT, E], BF16)
        xqT = sb("xqT", [P, EC, TOK], BF16)
        f_sb = sb("f_sb", [P, TT, E], BF16)
        fbias_sb = sb("fbias_sb", [P, TT, E], BF16)
        w_raw = score_sb[:, RING - 1, 0:EC, :]
        wT = [sb(f"wT{k}", [P, EC, E]) for k in range(4)]
        b_col = sb("b_col", [P, 3, EC])
        bo_row = sb("bo_row", [P, E])
        fb_row = sb("fb_row", [P, E], BF16)
        fk_sb = sb("fk_sb", [P, EC, E], BF16)
        kq_sb = sb("kq_sb", [P, EC, E], BF16)
        gates = sb("gates", [P, 2])
        tg = sb("tg", [P, 2])
        scl = sb("scl", [P, 2])
        rscl = sb("rscl", [P, 2])
        oscl = sb("oscl", [P, 1])
        half_c = sb("half_c", [P, TT])
        ident = sb("ident", [P, P])
        identb = sb("identb", [P, P], BF16)
        stat6 = [sb(f"stat6_{k}", [P, TT, 6]) for k in range(2)]
        mv = [sb(f"mv_{k}", [P, TT, 2]) for k in range(2)]
        var = [sb(f"var_{k}", [P, TT]) for k in range(2)]
        rstd = [sb(f"rstd_{k}", [P, TT]) for k in range(2)]
        nmr = [sb(f"nmr_{k}", [P, TT]) for k in range(2)]
        rowmax = sb("rowmax", [P, TT])
        nanrow = sb("nanrow", [P, TT])

        ps_s = ps("ps_s", [P, 2, 512])
        ps_t = ps("ps_t", [P, 2, 512])
        ps_o = ps("ps_o", [P, 512])
        ps_a = ps("ps_a", [P, 512])
        ps_b = ps("ps_b", [P, 512])
        ps_x = ps("ps_x", [P, 512])
        ps_xb = ps_x[:, 0:TOK].bitcast(BF16)

        s_carrier = sem("register_waits_carried")
        s_w = sem("weights_loaded")
        s_small = sem("small_loaded")
        s_wps = sem("weight_in_psum")
        s_wev = sem("weight_evacuated")
        s_id = sem("constants_ready")
        s_tanh = sem("tanh_done")
        s_init = sem("setup_steps")
        s_kq = sem("kernel_quantised")
        s_x = sem("x_loaded")
        s_ctx = sem("ctx_loaded")
        s_mv = [sem(f"moments_ready{k}") for k in range(2)]
        s_bn = [sem(f"halves_ready{k}") for k in range(2)]
        s_ln = [sem(f"layernorm_steps{k}") for k in range(2)]
        s_xn = [sem(f"normalised{k}") for k in range(2)]
        s_sp = sem("split_steps")
        s_ft = sem("front_transposed")
        s_fe = sem("front_evacuated")
        s_fp = sem("projection_in_psum")
        s_pe = sem("projection_evacuated")
        s_qd = sem("query_levels_in_dram")
        s_kd = sem("key_levels_in_dram")
        s_vd = sem("values_in_dram")
        s_od = sem("mixed_in_dram")
        s_t0 = sem("thresholds_started")
        s_upd = sem("update_steps")
        s_thr = sem("thresholds_moved")
        s_cnt = sem("counted_by_scalar")
        s_dcnt = sem("counted_by_vector")
        s_fin = sem("final_steps")
        s_flag = sem("unsure_rows_known")
        s_fsum = sem("unsure_rows_summed")
        s_load = sem("unsure_counts_ready")
        s_qm = sem("queries_moved")
        s_km = sem("keys_moved")
        s_qh = sem("queries_by_head")
        s_fv = sem("value_projection_in_psum")
        s_pv = sem("value_projection_evacuated")
        s_va = sem("values_ready")
        s_S = sem("scores_in_psum")
        s_copied = sem("scores_copied")
        s_step = sem("selection_steps")
        s_sel = sem("selected")
        s_exp = sem("exp_done")
        s_P = sem("probs_ready")
        s_T = sem("probs_transposed")
        s_PT = sem("probs_evacuated")
        s_PV = sem("values_mixed")
        s_O = sem("mixed_evacuated")
        s_Om = sem("mixed_moved")
        s_rec = sem("denominators_inverted")
        s_rd = sem("reciprocals_in_dram")
        s_rb = sem("reciprocals_spread")
        s_norm = sem("attention_normalised")
        s_xr = sem("residual_loaded")
        s_xg = sem("residual_prepared")
        s_op = sem("out_projected")
        s_x1 = sem("residual_updated")
        s_y = sem("scaled")
        s_yb = sem("exponent_taken")
        s_mg = sem("magic_ready")
        s_nan = sem("range_checked")
        s_add = sem("magic_added")
        s_q = sem("quantised")
        s_qt = sem("quantised_transposed")
        s_qe = sem("quantised_evacuated")
        s_fm = sem("ffn_in_psum")
        s_f = sem("ffn_evacuated")
        s_fb = sem("ffn_biased")
        s_res = sem("result_ready")
        s_out = sem("out_stored")

        def carry(eng):
            eng.sem_inc(s_carrier, 1)

        x_dram = x.rearrange("b (t p) e -> b p t e", p=P)
        ctx_dram = ctx_in.rearrange("b (t p) e -> b p t e", p=P)
        out_dram = out.rearrange("b (t p) e -> b p t e", p=P)
        QK_MOVES = len(Q_LEVELS) * 16
        O_MOVES = (EC + 1) * 16
        q_scr = nc.dram_tensor("q_scr", (3, E, TOK), BF16).ap()
        k_scr = nc.dram_tensor("k_scr", (3, E, TOK), BF16).ap()
        v_scr = nc.dram_tensor("v_scr", (TOK, E), F32).ap()
        o_scr = nc.dram_tensor("o_scr", (2 * D, NJ, TOK), F32).ap()
        r_scr = nc.dram_tensor("r_scr", (NJ, TOK), F32).ap()

        def one_run(ap):
            return ap.rearrange("j (a k) -> (j a) k", k=NJ * TOK // P)

        def one(ap, b):
            return ap[bass.ds(b, 1)].rearrange("b p t e -> p (b t) e")

        def schedule(eng, batch):
            for b in range(4):
                batch(b, b % 2, lambda d, b=b: 0 <= b + d < NB)
            with eng.Fori(4, NB - 4, 2) as i:
                batch(i, 0, lambda d: True)
                batch(i + 1, 1, lambda d: True)
            for b in range(NB - 4, NB):
                batch(b, b % 2, lambda d, b=b: 0 <= b + d < NB)

        block = stack.enter_context(nc.Block())

        @block.sync
        def _(sp):
            def load_front(b):
                sp.wait_ge(s_xn[0], at(b))
                carry(sp)
                sp.dma_start(x_in[:], one(x_dram, b)).then_inc(s_x, 16)
                sp.wait_ge(s_ft, at(b))
                carry(sp)
                sp.dma_start(ctx_sb[:], one(ctx_dram, b)).then_inc(s_ctx, 16)

            def move_operands(b, p):
                for k, (scr, dst, levels, stored, moved) in enumerate(((q_scr, q_rows, Q_LEVELS, s_qd, s_qm),
                                                                       (k_scr, ks[p], K_LEVELS, s_kd, s_km))):
                    sp.wait_ge(s_sp, 10 * b + 5 * k + 5)
                    carry(sp)
                    sp.wait_ge(moved, at(QK_MOVES * b))
                    carry(sp)
                    sp.dma_start(scr.rearrange("l (c p) t -> p (l c) t", p=P),
                                 split[k][:].rearrange("p l c t -> p (l c) t")).then_inc(stored, 16)
                    if k == 0:
                        sp.wait_ge(s_qh, at(b))
                    else:
                        sp.wait_ge(s_S, at(16 * (b - 1)))
                    carry(sp)
                    sp.wait_ge(stored, 16 * (b + 1))
                    carry(sp)
                    for s, lev in enumerate(levels):
                        sp.dma_start(dst[D * s:D * s + D], scr[lev].rearrange("(j d) t -> d j t", d=D)).then_inc(moved, 16)

            def move_values(b, p):
                sp.wait_ge(s_pv, b + 1)
                carry(sp)
                sp.wait_ge(s_va, at(16 * b))
                carry(sp)
                sp.dma_start(v_scr.rearrange("(t p) e -> p t e", p=P), proj[2][:]).then_inc(s_vd, 16)
                sp.wait_ge(s_PV, at(16 * (b - 1)))
                carry(sp)
                sp.wait_ge(s_vd, 16 * (b + 1))
                carry(sp)
                with nc.allow_non_contiguous_dma(reason="one key row of a head is 64 bytes"):
                    sp.dma_start(v_aug[p][:, :, 0:D],
                                 v_scr.rearrange("(k q) (j d) -> (q j) k d", q=8, d=D)).then_inc(s_va, 16)

            def move_out(b):
                sp.wait_ge(s_O, 4 * b + 4)
                carry(sp)
                sp.wait_ge(s_Om, at(O_MOVES * b))
                carry(sp)
                for c in range(4):
                    sp.dma_start(o_scr[:, :, 64 * c:64 * c + 64], o_sb[32 * c:32 * c + 32]).then_inc(s_od, 16)
                sp.wait_ge(s_op, at(b))
                carry(sp)
                sp.wait_ge(s_rec, at(b))
                carry(sp)
                sp.wait_ge(s_od, 64 * (b + 1))
                carry(sp)
                for c in range(EC):
                    sp.dma_start(attT[:, c, :],
                                 o_scr[0:D, 8 * c:8 * c + 8].rearrange("d j t -> j d t")).then_inc(s_Om, 16)
                sp.dma_start(den_sb[:], one_run(o_scr[D])).then_inc(s_Om, 16)

            def spread_reciprocals(b):
                sp.wait_ge(s_rec, b + 1)
                carry(sp)
                sp.wait_ge(s_rb, at(16 * EC * b))
                carry(sp)
                sp.dma_start(one_run(r_scr), rec_sb[:]).then_inc(s_rd, 16)
                sp.wait_ge(s_norm, at(b))
                carry(sp)
                sp.wait_ge(s_rd, 16 * (b + 1))
                carry(sp)
                for c in range(EC):
                    rows = r_scr[8 * c:8 * c + 8].rearrange("j (o t) -> j o t", o=1).to_broadcast([8, D, TOK])
                    sp.dma_start(recT[:, c, :], rows).then_inc(s_rb, 16)

            def store(b, p):
                sp.wait_ge(s_res, b + 1)
                carry(sp)
                sp.dma_start(one(out_dram, b), x_res[p][:]).then_inc(s_out, 16)
                sp.wait_ge(s_out, 16 * (b + 1))
                carry(sp)

            for k, w in enumerate((Wq, Wk, Wv, Wo)):
                sp.wait_ge(s_wps, at(k))
                sp.dma_start(w_raw, w.rearrange("(c p) i -> p c i", p=P)).then_inc(s_w, 16)
                if k == 0:
                    load_front(0)
            load_front(1)
            move_operands(0, 0)
            move_values(0, 0)
            move_operands(1, 1)
            load_front(2)

            def batch(b, p, has):
                if has(-2):
                    spread_reciprocals(b - 2)
                if has(3):
                    load_front(b + 3)
                if has(2):
                    move_operands(b + 2, p)
                if has(1):
                    move_values(b + 1, 1 - p)
                if has(-1):
                    move_out(b - 1)
                if has(-3):
                    store(b - 3, 1 - p)
                if has(-1):
                    sp.dma_start(x_res[1 - p][:], one(x_dram, b - 1)).then_inc(s_xr, 16)

            schedule(sp, batch)
            spread_reciprocals(NB - 2)
            store(NB - 3, 1)
            sp.dma_start(x_res[1][:], one(x_dram, NB - 1)).then_inc(s_xr, 16)
            move_out(NB - 1)
            spread_reciprocals(NB - 1)
            for b in (NB - 2, NB - 1):
                store(b, b % 2)

        @block.gpsimd
        def _(pool):
            nc.gpsimd.memset(ident[:], 0.0).then_inc(s_id, 1)
            pool.wait_ge(s_id, 1)
            nc.gpsimd.affine_select(out=ident[:], in_=ident[:], compare_op=ALU.not_equal, fill=1.0, base=0,
                                    pattern=[[-1, P]], channel_multiplier=1).then_inc(s_id, 1)
            pool.wait_ge(s_id, 2)
            nc.gpsimd.tensor_copy(identb[:], ident[:]).then_inc(s_id, 1)
            for p in range(2):
                nc.gpsimd.memset(v_aug[p][:, :, D:2 * D], 1.0).then_inc(s_id, 1)
            nc.gpsimd.memset(half_c[:], -0.5).then_inc(s_id, 1)
            nc.gpsimd.memset(minus_twos[:], -2.0).then_inc(s_id, 1)
            nc.gpsimd.memset(ones_c[:], 1.0).then_inc(s_id, 1)
            nc.gpsimd.memset(ones_r[:], 1.0).then_inc(s_id, 1)
            nc.gpsimd.memset(aim[:, 0:ACT_TILES], TOK - 2 * AIM).then_inc(s_id, 1)
            nc.gpsimd.memset(aim[:, ACT_TILES:GT], -2 * AIM).then_inc(s_id, 1)
            for t in range(GT):
                nc.gpsimd.memset(numbers[:, t:t + 1], float(t + 1)).then_inc(s_id, 1)
            for r in range(WINDOW):
                nc.gpsimd.memset(ranks[:, r:r + 1], float(TOPK - r)).then_inc(s_id, 1)
            with nc.allow_non_contiguous_dma(reason="small vectors"):
                for k, v in enumerate((bq, bk, bv)):
                    pool.dma_start(b_col[:, k, :], v.rearrange("(c p) -> p c", p=P)).then_inc(s_small, 16)
                pool.dma_start(bv_row[:], bv.rearrange("(o n) -> o n", o=1)).then_inc(s_small, 16)
                for dst, v in ((bo_row, bo), (fb_row, fb)):
                    pool.dma_start(dst[:], v.rearrange("(o n) -> o n", o=1).to_broadcast([P, E])).then_inc(s_small, 16)
                for k, v in enumerate((g_x, g_f)):
                    pool.dma_start(gates[:, k:k + 1], v.rearrange("(o n) -> o n", o=1).to_broadcast([P, 1])).then_inc(s_small, 16)
                for k, v in enumerate((s_in, s_k)):
                    pool.dma_start(scl[:, k:k + 1], v.rearrange("(o n) -> o n", o=1).to_broadcast([P, 1])).then_inc(s_small, 16)
                pool.dma_start(fk_sb[:], fk.rearrange("(c p) n -> p c n", p=P)).then_inc(s_small, 16)
            pool.wait_ge(s_id, 35)

            def layernorm(b, k, src, dst):
                pool.wait_ge(s_mv[k], b + 1)
                carry(pool)
                nc.gpsimd.tensor_scalar(var[k][:], mv[k][:, :, 1], EPS, None, ALU.add).then_inc(s_ln[k], 1)
                pool.wait_ge(s_ln[k], 4 * b + 1)
                nc.gpsimd.tensor_tensor(rstd[k][:], var[k][:], half_c[:], ALU.pow).then_inc(s_ln[k], 1)
                pool.wait_ge(s_ln[k], 4 * b + 2)
                nc.gpsimd.tensor_tensor(nmr[k][:], mv[k][:, :, 0], rstd[k][:], ALU.mult).then_inc(s_ln[k], 1)
                pool.wait_ge(s_ln[k], 4 * b + 3)
                carry(pool)
                nc.gpsimd.tensor_scalar(nmr[k][:], nmr[k][:], -1.0, None, ALU.mult).then_inc(s_ln[k], 1)
                pool.wait_ge(s_ln[k], 4 * b + 4)
                carry(pool)
                for t in range(TT):
                    ins = nc.gpsimd.tensor_scalar(dst[:, t, :], src[:, t, :], rstd[k][:, t:t + 1], nmr[k][:, t:t + 1],
                                                  ALU.mult, ALU.add)
                ins.then_inc(s_xn[k], 1)

            def front_layernorm(b):
                pool.wait_ge(s_ft, at(b))
                layernorm(b, 0, x_in, xn_sb)

            def split_operands(b):
                for k in range(2):
                    pool.wait_ge((s_qm, s_km)[k], at(QK_MOVES * b))
                    pool.wait_ge(s_pe, at(2 * b + 1 + k))
                    carry(pool)
                    base = 10 * b + 5 * k
                    hi, mid, lo = (split[k][:, lev] for lev in range(3))
                    nc.gpsimd.tensor_copy(hi, proj[k][:]).then_inc(s_sp, 1)
                    pool.wait_ge(s_sp, base + 1)
                    nc.gpsimd.tensor_tensor(rest[:], proj[k][:], hi, ALU.subtract).then_inc(s_sp, 1)
                    pool.wait_ge(s_sp, base + 2)
                    carry(pool)
                    nc.gpsimd.tensor_copy(mid, rest[:]).then_inc(s_sp, 1)
                    pool.wait_ge(s_sp, base + 3)
                    nc.gpsimd.tensor_tensor(rest[:], rest[:], mid, ALU.subtract).then_inc(s_sp, 1)
                    pool.wait_ge(s_sp, base + 4)
                    carry(pool)
                    nc.gpsimd.tensor_copy(lo, rest[:]).then_inc(s_sp, 1)
                    pool.wait_ge(s_sp, base + 5)

            def normalise_attention(b, p):
                pool.wait_ge(s_xr, 16 * (b + 1))
                for t in range(TT):
                    ins = nc.gpsimd.tensor_tensor(x_res[p][:, t, :], x_res[p][:, t, :], bo_row[:], ALU.add)
                ins.then_inc(s_xg, 1)
                pool.wait_ge(s_rb, 16 * EC * (b + 1))
                pool.wait_ge(s_Om, O_MOVES * (b + 1))
                nc.gpsimd.tensor_tensor(attT[:], attT[:], recT[:], ALU.mult).then_inc(s_norm, 1)

            def second_layernorm(b, p):
                pool.wait_ge(s_y, at(b))
                carry(pool)
                layernorm(b, 1, x_res[p], xb_sb)

            def round_tokens(b):
                pool.wait_ge(s_mg, b + 1)
                nc.gpsimd.tensor_tensor(ysum_sb[:], y_sb[:], magic_sb[:], ALU.add).then_inc(s_add, 1)
                pool.wait_ge(s_add, b + 1)
                pool.wait_ge(s_qt, at(b))
                nc.gpsimd.tensor_tensor(xq_sb[:], ysum_sb[:], magic_sb[:], ALU.subtract).then_inc(s_q, 1)

            front_layernorm(0)
            split_operands(0)
            front_layernorm(1)
            split_operands(1)
            front_layernorm(2)

            def batch(b, p, has):
                if has(-3):
                    round_tokens(b - 3)
                if has(-2):
                    normalise_attention(b - 2, p)
                if has(2):
                    split_operands(b + 2)
                if has(-2):
                    second_layernorm(b - 2, p)
                if has(3):
                    front_layernorm(b + 3)

            pool.wait_ge(s_init, 3)
            schedule(pool, batch)
            round_tokens(NB - 3)
            for b in (NB - 2, NB - 1):
                normalise_attention(b, b % 2)
                second_layernorm(b, b % 2)
                round_tokens(b)

        @block.tensor
        def _(pe):
            pe.wait_ge(s_id, 35)
            for k in range(4):
                pe.wait_ge(s_w, 16 * (k + 1))
                pe.wait_ge(s_wev, at(k))
                for ic in range(EC):
                    for oc in range(EC):
                        ins = nc.tensor.transpose(ps_a[:, ic * E + oc * P:ic * E + oc * P + P],
                                                  w_raw[:, oc, ic * P:ic * P + P], ident[:])
                ins.then_inc(s_wps, 1)
            pe.wait_ge(s_wev, 4)

            def front_transposes(b):
                pe.wait_ge(s_xn[0], b + 1)
                pe.wait_ge(s_ctx, 16 * b + 16)
                pe.wait_ge(s_pv, at(b))
                pe.wait_ge(s_pe, at(2 * b))
                for dst, src in ((ps_a, xn_sb), (ps_b, ctx_sb)):
                    for c in range(EC):
                        for t in range(TT):
                            ins = nc.tensor.transpose(dst[:, c * TOK + t * P:c * TOK + t * P + P],
                                                      src[:, t, c * P:c * P + P], ident[:])
                ins.then_inc(s_ft, 1)

            def project(b, k):
                if k == 0:
                    pe.wait_ge(s_fe, 2 * b + 2)
                dst, src = ((ps_a, xT), (ps_b, cT))[k]
                for oc in range(EC):
                    for ic in range(EC):
                        ins = nc.tensor.matmul(dst[:, oc * TOK:(oc + 1) * TOK], wT[k][:, ic, oc * P:oc * P + P],
                                               src[:, ic, :], start=(ic == 0), stop=(ic == EC - 1))
                ins.then_inc(s_fp, 1)

            def project_values(b):
                pe.wait_ge(s_pe, 2 * b + 1)
                for t in range(TT):
                    for ic in range(EC):
                        nc.tensor.matmul(ps_a[:, t * E:(t + 1) * E], cT[:, ic, t * P:(t + 1) * P], wT[2][:, ic, :],
                                         start=(ic == 0), stop=False)
                    ins = nc.tensor.matmul(ps_a[:, t * E:(t + 1) * E], ones_r[:], bv_row[:], start=False, stop=True)
                ins.then_inc(s_fv, 1)

            def scores(b, p, g, n):
                H = 16 * b + GH * g + n
                h = head_of(g, n)
                if g == 0 and n == 0:
                    pe.wait_ge(s_qh, b + 1)
                    pe.wait_ge(s_km, QK_MOVES * (b + 1))
                pe.wait_ge(s_copied, at(H - 1))
                for jh in range(2):
                    ins = nc.tensor.matmul(ps_s[:, n % 2, jh * TOK:(jh + 1) * TOK],
                                           qs[p][:, h, 8 * jh:8 * jh + 8, :].rearrange("d j t -> d (j t)"),
                                           ks[p][:, :, D * h:D * h + D], start=True, stop=True)
                ins.then_inc(s_S, 1)

            def prob_transposes(i, n):
                H = GH * i + n
                pe.wait_ge(s_P, H + 1)
                pe.wait_ge(s_PT, at(H - 1))
                for kc in range(2):
                    for jh in range(2):
                        ins = nc.tensor.transpose(ps_t[:, n % 2, kc * TOK + jh * P:kc * TOK + jh * P + P],
                                                  p_sb[:, n % 2, jh, kc * P:kc * P + P], ident[:])
                ins.then_inc(s_T, 1)

            def mix(b, p, g, n):
                H = 16 * b + GH * g + n
                c, half = n % 4, n // 4
                h = head_of(g, n)
                if g == 0 and n == 0:
                    pe.wait_ge(s_va, 16 * (b + 1))
                pe.wait_ge(s_PT, H + 1)
                if c == 0:
                    pe.wait_ge(s_O, at(4 * b + 2 * g + half))
                for kc in range(2):
                    ins = nc.tensor.matmul(ps_o[32 * c:32 * c + 32, half * TOK:(half + 1) * TOK],
                                           v_aug[p][:, 2 * h + kc, :], pT_sb[:, n % 2, kc * TOK:(kc + 1) * TOK],
                                           start=(kc == 0), stop=(kc == 1), tile_position=(0, 32 * c))
                ins.then_inc(s_PV, 1)

            def out_project(b, sums):
                pe.wait_ge(s_norm, b + 1)
                pe.wait_ge(s_load, 2 * sums)
                pe.wait_ge(s_f, at(b))
                for t in range(TT):
                    for c in range(EC):
                        ins = nc.tensor.matmul(ps_x[:, t * E:(t + 1) * E], attT[:, c, t * P:t * P + P], wT[3][:, c, :],
                                               start=(c == 0), stop=(c == EC - 1))
                ins.then_inc(s_op, 1)

            def ffn_transposes(b, sums):
                pe.wait_ge(s_load, 2 * sums)
                pe.wait_ge(s_x1, b + 1)
                pe.wait_ge(s_q, b + 1)
                for c in range(EC):
                    for t in range(TT):
                        ins = nc.tensor.transpose(ps_xb[:, c * TOK + t * P:c * TOK + t * P + P],
                                                  xq_sb[:, t, c * P:c * P + P], identb[:])
                ins.then_inc(s_qt, 1)

            def ffn_matmul(b):
                pe.wait_ge(s_qe, b + 1)
                pe.wait_ge(s_kq, 1)
                for t in range(TT):
                    for c in range(EC):
                        ins = nc.tensor.matmul(ps_x[:, t * E:(t + 1) * E], xqT[:, c, t * P:t * P + P], kq_sb[:, c, :],
                                               start=(c == 0), stop=(c == EC - 1))
                ins.then_inc(s_fm, 1)

            def sum_unsure(i, updated, fed):
                pe.wait_ge(s_x1, at(updated))
                pe.wait_ge(s_f, at(fed))
                pe.wait_ge(s_flag, i + 1)
                nc.tensor.matmul(ps_x[0:1, 0:GT], ones_c[:], unsure_b[:], start=True, stop=True).then_inc(s_fsum, 1)

            for b in range(2):
                front_transposes(b)
                project(b, 0)
                project(b, 1)
                if b == 0:
                    project_values(0)
            for g in range(2):
                for n in range(GH):
                    scores(0, 0, g, n)
            scores(1, 1, 0, 0)

            def mix_stage(b, p, g, n, before):
                h = earlier(b, p, g, n, MASK_LAG, before)
                if h:
                    prob_transposes(2 * h[0] + h[2], h[3])
                h = earlier(b, p, g, n, MIX_LAG, before)
                if h:
                    mix(*h)

            def batch(b, p, has):
                for g in range(2):
                    mb, mp, mg = (b - 1, 1 - p, 1) if g == 0 else (b, p, 0)
                    mixes = g == 1 or has(-1)
                    if mixes:
                        sum_unsure(2 * mb + mg, b - 2, b - 2 if g else b - 3)
                    for n in range(GH):
                        if has(1) and (g, n) != (1, GH - 1):
                            scores(b + 1, 1 - p, *divmod(GH * g + n + 1, GH))
                        if has(2) and (g, n) == (1, GH - 1):
                            scores(b + 2, p, 0, 0)
                        if mixes:
                            mix_stage(mb, mp, mg, n, has(-1))
                        if has(1) and (g, n) == (0, 0):
                            project_values(b + 1)
                        if has(2) and (g, n) == (0, 2):
                            front_transposes(b + 2)
                        if has(2) and (g, n) == (0, 4):
                            project(b + 2, 0)
                        if has(2) and (g, n) == (0, 6):
                            project(b + 2, 1)
                        if has(-3) and (g, n) == (0, 3):
                            ffn_transposes(b - 3, 2 * b)
                        if has(-3) and (g, n) == (0, 5):
                            ffn_matmul(b - 3)
                        if has(-2) and (g, n) == (1, 2):
                            out_project(b - 2, 2 * b + 1)

            schedule(pe, batch)
            sum_unsure(2 * NB - 1, NB - 2, NB - 3)
            for n in range(GH):
                mix_stage(NB - 1, 1, 1, n, True)
                if n == 3:
                    ffn_transposes(NB - 3, 2 * NB)
                if n == 5:
                    ffn_matmul(NB - 3)
                if n == 7:
                    out_project(NB - 2, 2 * NB)
            for n in range(GH - MASK_LAG, GH):
                prob_transposes(2 * NB - 1, n)
                mix(NB - 1, 1, 1, n - MASK_LAG)
            for n in range(GH - MASK_LAG, GH):
                mix(NB - 1, 1, 1, n)
            for b in (NB - 2, NB - 1):
                if b == NB - 1:
                    out_project(b, 2 * NB)
                ffn_transposes(b, 2 * NB)
                ffn_matmul(b)

        @block.scalar
        def _(act):
            for k in range(4):
                act.wait_ge(s_wps, k + 1)
                nc.scalar.copy(wT[k][:].rearrange("p c e -> p (c e)"), ps_a[:]).then_inc(s_wev, 1)
            act.wait_ge(s_small, 16 * 11)
            nc.scalar.activation(tg[:], gates[:], ACT.Tanh).then_inc(s_tanh, 1)

            def evacuate_front(b):
                act.wait_ge(s_ft, b + 1)
                act.wait_ge(s_fp, at(2 * b))
                act.wait_ge(s_fv, at(b))
                nc.scalar.copy(xT[:].rearrange("p c t -> p (c t)"), ps_a[:]).then_inc(s_fe, 1)
                nc.scalar.copy(cT[:].rearrange("p c t -> p (c t)"), ps_b[:]).then_inc(s_fe, 1)

            def evacuate_projection(b, k):
                act.wait_ge(s_fp, 2 * b + k + 1)
                act.wait_ge(s_sp, at(10 * (b - 1) + 5 + 5 * k))
                src = (ps_a, ps_b)[k]
                for c in range(EC):
                    ins = nc.scalar.activation(proj[k][:, c, :], src[:, c * TOK:(c + 1) * TOK], ACT.Identity,
                                               bias=b_col[:, k, c:c + 1], scale=(D ** -0.5 if k == 0 else 1.0))
                ins.then_inc(s_pe, 1)

            def queries_by_head(b, p):
                act.wait_ge(s_qm, QK_MOVES * (b + 1))
                act.wait_ge(s_S, at(16 * (b - 1)))
                nc.scalar.copy(qs[p][:].rearrange("d h j t -> d j h t"),
                               q_rows[:].rearrange("d j (h t) -> d j h t", t=D)).then_inc(s_qh, 1)

            def evacuate_values(b):
                act.wait_ge(s_fv, b + 1)
                act.wait_ge(s_vd, at(16 * b))
                nc.scalar.copy(proj[2][:].rearrange("p t e -> p (t e)"), ps_a[:]).then_inc(s_pv, 1)

            def guide_counts(i, slot, r):
                act.wait_ge(s_cnt, at(GUIDES * i + r))
                act.wait_ge(s_thr, GUIDES * i + r + 1)
                for t in range(ACT_TILES):
                    ins = nc.scalar.activation(act_junk[:, t, :], score_sb[:, slot, t, :], ACT.Sign, scale=-1.0,
                                               bias=X[slot % 2][:, 0, t:t + 1], accum_out=count[slot % 2][:, t:t + 1])
                ins.then_inc(s_cnt, 1)

            def exps(i, slot, n):
                H = GH * i + n
                act.wait_ge(s_sel, i + 1)
                act.wait_ge(s_P, at(H - 1))
                for jh in range(2):
                    t = 2 * n + jh
                    ins = nc.scalar.activation(e_sb[:, n % 2, jh, :], score_sb[:, slot, t, :], ACT.Exp,
                                               bias=nmx[:, slot, t:t + 1])
                ins.then_inc(s_exp, 1)

            def evacuate_probs(i, n):
                H = GH * i + n
                act.wait_ge(s_T, H + 1)
                act.wait_ge(s_PV, at(H - 1))
                nc.scalar.copy(pT_sb[:, n % 2, :], ps_t[:, n % 2, :]).then_inc(s_PT, 1)

            def evacuate_mixed(b, p, g, half):
                if g == 0 and half == 0:
                    act.wait_ge(s_Om, at(O_MOVES * b))
                act.wait_ge(s_PV, 16 * b + 8 * g + 4 * half + 4)
                q = 2 * g + half
                nc.scalar.copy(o_sb[:, :, D * q:D * q + D],
                               ps_o[:, half * TOK:(half + 1) * TOK].rearrange("p (j t) -> p j t", t=D)).then_inc(s_O, 1)

            def evacuate_quantised(b):
                act.wait_ge(s_qt, b + 1)
                act.wait_ge(s_fm, at(b))
                nc.scalar.copy(xqT[:].rearrange("p c t -> p (c t)"), ps_xb).then_inc(s_qe, 1)

            def evacuate_ffn(b):
                act.wait_ge(s_fm, b + 1)
                act.wait_ge(s_fb, at(b))
                nc.scalar.activation(f_sb[:].rearrange("p t e -> p (t e)"), ps_x[:], ACT.Copy, scale=oscl[:]).then_inc(s_f, 1)

            act.wait_ge(s_init, 3)
            act.wait_ge(s_id, 35)
            for b in range(2):
                evacuate_front(b)
                evacuate_projection(b, 0)
                evacuate_projection(b, 1)
                if b == 0:
                    evacuate_values(0)
            for b in range(2):
                queries_by_head(b, b)

            def after_transposes(b, p, g, n, before):
                if n % 4 == 0 and before:
                    done = earlier(b, p, g, n, GH, before)
                    evacuate_mixed(done[0], done[1], done[2], n // 4)
                h = earlier(b, p, g, n, MIX_LAG, before)
                if h:
                    evacuate_probs(2 * h[0] + h[2], h[3])

            def batch(b, p, has):
                for g in range(2):
                    mb, mp, mg = (b - 1, 1 - p, 1) if g == 0 else (b, p, 0)
                    mixes = g == 1 or has(-1)
                    guided = g == 0 or has(1)
                    for r in range(GUIDES):
                        if guided:
                            guide_counts(2 * b + g + 1, (2 * p + g + 1) % RING, r)
                        for n in (2 * r, 2 * r + 1):
                            if mixes:
                                after_transposes(mb, mp, mg, n, has(-1))
                                exps(2 * mb + mg, 2 * mp + mg, n)
                            if has(1) and (g, n) == (0, 2):
                                evacuate_values(b + 1)
                            if has(2) and (g, n) == (0, 4):
                                evacuate_front(b + 2)
                            if has(2) and (g, n) == (0, 6):
                                evacuate_projection(b + 2, 0)
                            if has(2) and (g, n) == (1, 0):
                                evacuate_projection(b + 2, 1)
                            if has(2) and (g, n) == (1, 5):
                                queries_by_head(b + 2, p)
                            if has(-3) and (g, n) == (0, 5):
                                evacuate_quantised(b - 3)
                            if has(-3) and (g, n) == (0, 7):
                                evacuate_ffn(b - 3)

            for r in range(GUIDES):
                guide_counts(0, 0, r)
            schedule(act, batch)
            for n in range(GH):
                after_transposes(NB - 1, 1, 1, n, True)
                exps(2 * NB - 1, RING - 1, n)
                if n == 5:
                    evacuate_quantised(NB - 3)
                if n == 7:
                    evacuate_ffn(NB - 3)
            evacuate_mixed(NB - 1, 1, 1, 0)
            for n in range(GH - MIX_LAG, GH):
                evacuate_probs(2 * NB - 1, n)
            evacuate_mixed(NB - 1, 1, 1, 1)
            for b in (NB - 2, NB - 1):
                evacuate_quantised(b)
                evacuate_ffn(b)

        @block.vector
        def _(dve):
            def moments(b, k, src):
                dve.wait_ge(s_xn[k], at(b))
                for t in range(TT):
                    nc.vector.bn_stats(stat6[k][:, t, :], src[:, t, :]).then_inc(s_bn[k], 1)
                dve.wait_ge(s_bn[k], at(TT * b + TT))
                carry(dve)
                for t in range(TT):
                    ins = nc.vector.bn_aggr(mv[k][:, t, :], stat6[k][:, t, :])
                ins.then_inc(s_mv[k], 1)

            def front_moments(b):
                dve.wait_ge(s_x, 16 * (b + 1))
                moments(b, 0, x_in)

            front_moments(0)
            dve.wait_ge(s_small, 16 * 11)
            nc.vector.tensor_scalar(b_col[:, 0, :], b_col[:, 0, :], D ** -0.5, None, ALU.mult).then_inc(s_init, 1)
            nc.vector.tensor_tensor(oscl[:], scl[:, 0:1], scl[:, 1:2], ALU.mult).then_inc(s_init, 1)
            dve.wait_ge(s_tanh, 1)
            nc.vector.tensor_scalar(bo_row[:], bo_row[:], tg[:, 0:1], None, ALU.mult).then_inc(s_init, 1)
            nc.vector.reciprocal(rscl[:], scl[:]).then_inc(s_init, 1)
            dve.wait_ge(s_init, 4)

            def exponent(dst, src):
                return nc.vector.tensor_scalar(dst.bitcast(I32), src.bitcast(I32), 0x7F800000, None, ALU.bitwise_and)

            def magnitude(dst, src):
                return nc.vector.tensor_scalar(dst.bitcast(I32), src.bitcast(I32), 0x7FFFFFFF, None, ALU.bitwise_and)

            def magic(dst):
                return nc.vector.tensor_scalar(dst, dst, 2.0 ** -6, 1.5 * 2.0 ** 20, ALU.max, ALU.mult)

            def link(ins, value):
                ins.then_inc(s_init, 1)
                dve.wait_ge(s_init, at(value))

            link(nc.vector.tensor_scalar(y_sb[:], fk_sb[:], rscl[:, 1:2], None, ALU.mult), 5)
            link(exponent(magic_sb[:], y_sb[:]), 6)
            link(magic(magic_sb[:]), 7)
            link(nc.vector.tensor_tensor(ysum_sb[:], y_sb[:], magic_sb[:], ALU.add), 8)
            link(nc.vector.tensor_tensor(y_sb[:], ysum_sb[:], magic_sb[:], ALU.subtract), 9)
            link(magnitude(yabs_sb[:], y_sb[:]), 10)
            link(nc.vector.tensor_scalar(ysum_sb[:], yabs_sb[:], 448.0, 3.0e38, ALU.is_gt, ALU.mult), 11)
            link(nc.vector.tensor_scalar(ysum_sb[:], ysum_sb[:], 3.0e38, None, ALU.mult), 12)
            link(nc.vector.tensor_tensor(magic_sb[:], ysum_sb[:], ysum_sb[:], ALU.subtract), 13)
            nc.vector.tensor_tensor(kq_sb[:], y_sb[:], magic_sb[:], ALU.add).then_inc(s_kq, 1)
            dve.wait_ge(s_kq, 1)

            def copy_scores(i, slot, n, jh):
                H = GH * i + n
                if jh == 0:
                    dve.wait_ge(s_S, H + 1)
                t = 2 * n + jh
                src = ps_s[:, n % 2, jh * TOK:(jh + 1) * TOK].rearrange("p (j t) -> p t j", t=D)
                dst = score_sb[:, slot, t, :].rearrange("p (t j) -> p t j", j=NJ)
                ins = nc.vector.tensor_scalar(dst, src, 0.0, None, ALU.add, ALU.max, accum_out=mx[:, slot, t:t + 1])
                if jh == 1:
                    ins.then_inc(s_copied, 1)

            def start_thresholds(i, slot):
                x = X[slot % 2]
                dve.wait_ge(s_copied, GH * i + GH)
                carry(dve)
                dve.wait_ge(s_thr, at(GUIDES * i))
                carry(dve)
                nc.vector.tensor_scalar(nmx[:, slot, :], mx[:, slot, :], -1.0, None, ALU.mult)
                nc.vector.tensor_scalar(x[:, 0, :], mx[:, slot, :], START, None, ALU.mult).then_inc(s_thr, 1)
                nc.vector.memset(A[slot % 2][:], NO_POINT)
                nc.vector.memset(B[slot % 2][:], -NO_POINT).then_inc(s_t0, 1)
                dve.wait_ge(s_t0, i + 1)
                carry(dve)

            def guide_counts(i, slot, r):
                dve.wait_ge(s_thr, GUIDES * i + r + 1)
                for t in range(ACT_TILES, GT):
                    ins = nc.vector.scalar_tensor_tensor(dve_junk[:, t - ACT_TILES, :], score_sb[:, slot, t, :],
                                                         X[slot % 2][:, 0, t:t + 1], minus_twos[:], ALU.is_gt, ALU.mult, accum_out=count[slot % 2][:, t:t + 1])
                ins.then_inc(s_dcnt, 1)

            def update_thresholds(i, slot, r):
                x = X[slot % 2]
                lo_side, hi_side = A[slot % 2], B[slot % 2]
                off = x[:, 1:2, :].to_broadcast([P, 2, GT])
                dve.wait_ge(s_cnt, GUIDES * i + r + 1)
                carry(dve)
                dve.wait_ge(s_dcnt, GUIDES * i + r + 1)
                carry(dve)
                nc.vector.tensor_tensor(x[:, 1, :], aim[:], count[slot % 2][:], ALU.subtract).then_inc(s_upd, 1)
                yield
                dve.wait_ge(s_upd, 1)
                nc.vector.tensor_scalar(above[:], off, 0.0, None, ALU.is_gt)
                nc.vector.tensor_scalar(below[:], off, 0.0, None, ALU.is_le)
                nc.vector.tensor_tensor(square[:], x[:, 1, :], x[:, 1, :], ALU.mult)
                nc.vector.scalar_tensor_tensor(newton[:], x[:, 1, :], SLOPE, mx[:, slot, :], ALU.mult,
                                               ALU.mult).then_inc(s_upd, 1)
                yield
                dve.wait_ge(s_upd, 2)
                nc.vector.copy_predicated(lo_side[:], above[:], x[:])
                nc.vector.copy_predicated(hi_side[:], below[:], x[:])
                nc.vector.tensor_tensor(newton[:], newton[:], x[:, 0, :], ALU.add)
                if r:
                    nc.vector.tensor_scalar(far_f[:], square[:], (WINDOW - 1) ** 2 + 0.5, None, ALU.is_gt)
                nc.vector.tensor_scalar(far[:], square[:], (WINDOW - 1) ** 2 + 0.5, None, ALU.is_gt).then_inc(s_upd, 1)
                yield
                dve.wait_ge(s_upd, 3)
                ins = nc.vector.copy_predicated(x[:, 0, :], far[:], newton[:])
                if r == 0:
                    ins.then_inc(s_thr, 1)
                    dve.sem_clear(s_upd)
                    return
                nc.vector.tensor_tensor(AB[:], hi_side[:], lo_side[:], ALU.subtract).then_inc(s_upd, 1)
                yield
                dve.wait_ge(s_upd, 4)
                nc.vector.reciprocal(chord[:], AB[:, 1, :])
                nc.vector.tensor_tensor(product[:], AB[:, 0, :], lo_side[:, 1, :], ALU.mult)
                nc.vector.scalar_tensor_tensor(both[:], AB[:, 1, :], -NO_POINT + TOK, far_f[:], ALU.is_gt,
                                               ALU.mult).then_inc(s_upd, 1)
                yield
                dve.wait_ge(s_upd, 5)
                nc.vector.tensor_tensor(chord[:], chord[:], product[:], ALU.mult).then_inc(s_upd, 1)
                yield
                dve.wait_ge(s_upd, 6)
                nc.vector.tensor_tensor(chord[:], lo_side[:, 0, :], chord[:], ALU.subtract).then_inc(s_upd, 1)
                yield
                dve.wait_ge(s_upd, 7)
                ins = nc.vector.copy_predicated(x[:, 0, :], both[:], chord[:])
                if r < GUIDES - 1:
                    ins.then_inc(s_thr, 1)
                    dve.sem_clear(s_upd)
                else:
                    ins.then_inc(s_upd, 1)
                    yield
                    dve.wait_ge(s_upd, 8)
                    dve.sem_clear(s_upd)

            FINAL = 2 * GT + GUIDES + 7

            def final_tiles(i, slot, q):
                tiles = range(q * QUARTER, (q + 1) * QUARTER)
                base = FINAL * i + (2 * QUARTER + 1) * q + (q > 0)
                dve.wait_ge(s_fin, at(base))
                carry(dve)
                if q == 0:
                    nc.vector.tensor_copy(following[:, :, 0], X[slot % 2][:, 0, :]).then_inc(s_fin, 1)
                    base += 1
                for k, t in enumerate(tiles):
                    nc.vector.tensor_scalar(masked[:, k, :], score_sb[:, slot, t, :], X[slot % 2][:, 0, t:t + 1], None,
                                            ALU.is_gt, ALU.add, accum_out=final_count[:, t:t + 1]).then_inc(s_fin, 1)
                yield
                dve.wait_ge(s_fin, base + QUARTER)
                scores = score_sb[:, slot, q * QUARTER:(q + 1) * QUARTER, :]
                nc.vector.scalar_tensor_tensor(masked[:], masked[:], -BIG, scores,
                                               ALU.mult, ALU.add).then_inc(s_fin, 1)
                yield
                dve.wait_ge(s_fin, base + QUARTER + 1)
                carry(dve)
                for k, t in enumerate(tiles):
                    nc.vector.max(following[:, t, 1:], masked[:, k, :]).then_inc(s_fin, 1)

            def final_thresholds(i, slot):
                base = FINAL * i + 2 * GT + GUIDES + 1
                dve.wait_ge(s_fin, base)
                counts = final_count[:].rearrange("p (t o) -> p t o", o=1).to_broadcast([P, GT, WINDOW])
                places = ranks[:].rearrange("p (o r) -> p o r", o=1).to_broadcast([P, GT, WINDOW])
                nc.vector.tensor_tensor(place[:], counts, places, ALU.is_equal).then_inc(s_fin, 1)
                yield
                dve.wait_ge(s_fin, base + 1)
                nc.vector.tensor_tensor(pick[:], place[:], following[:, :, 0:WINDOW], ALU.mult).then_inc(s_fin, 1)
                nc.vector.tensor_tensor(pick65[:], place[:], following[:, :, 1:1 + WINDOW], ALU.mult).then_inc(s_fin, 1)
                yield
                dve.wait_ge(s_fin, base + 3)
                nc.vector.tensor_reduce(s64[:], pick[:], AX.X, ALU.add).then_inc(s_fin, 1)
                nc.vector.tensor_reduce(s65[:], pick65[:], AX.X, ALU.add).then_inc(s_fin, 1)
                yield
                dve.wait_ge(s_fin, base + 5)
                nc.vector.tensor_copy(thr[:, slot, :], s64[:]).then_inc(s_fin, 1)
                nc.vector.tensor_tensor(unsure_b[:], s64[:], s65[:], ALU.is_le).then_inc(s_flag, 1)

            def select_tile(slot, t):
                s = score_sb[:, slot, bass.ds(t, 1), :].rearrange("p o k -> p (o k)")
                rest_of = work[:, 0, :]
                nc.vector.tensor_scalar(thr[:, slot, bass.ds(t, 1)], thr[:, slot, bass.ds(t, 1)], 0.0, -BIG / 2,
                                        ALU.mult, ALU.add)
                nc.vector.tensor_copy(rest_of, s).then_inc(s_step, 1)
                for r in range(ROUNDS):
                    dve.wait_ge(s_step, 2 * r + 1)
                    nc.vector.max(max8[:], rest_of).then_inc(s_step, 1)
                    dve.wait_ge(s_step, 2 * r + 2)
                    nc.vector.match_replace(rest_of, max8[:], rest_of, -BIG).then_inc(s_step, 1)
                dve.wait_ge(s_step, 2 * ROUNDS + 1)
                nc.vector.tensor_scalar(work[:, 1, :], work[:, 0, :], -BIG / 2, -BIG, ALU.is_gt, ALU.mult).then_inc(s_step, 1)
                dve.wait_ge(s_step, 2 * ROUNDS + 2)
                nc.vector.tensor_tensor(s, s, work[:, 1, :], ALU.add).then_inc(s_step, 1)
                dve.wait_ge(s_step, 2 * ROUNDS + 3)
                dve.sem_clear(s_step)

            def read_unsure(i):
                dve.wait_ge(s_fsum, i + 1)
                carry(dve)
                nc.vector.tensor_scalar(unsure_f[:, 0:GT], ps_x[0:1, 0:GT], 0.0, None, ALU.add, ALU.add,
                                        accum_out=unsure_f[:, GT:GT + 1]).then_inc(s_load, 1)

            def convert_unsure(i):
                dve.wait_ge(s_load, 2 * i + 1)
                carry(dve)
                nc.vector.tensor_copy(unsure_i[:], unsure_f[:, GT:GT + 1]).then_inc(s_load, 1)

            def settle(i, slot):
                dve.wait_ge(s_load, 2 * i + 2)
                carry(dve)
                total = dve.value_load(unsure_i[0:1, 0:1], min_val=0, max_val=GT * P)
                with dve.If(total > 0):
                    done = [0]

                    def step(ins):
                        done[0] += 1
                        ins.then_inc(s_step, 1)
                        dve.wait_ge(s_step, done[0])

                    step(nc.vector.tensor_scalar(marked[:, 0:GT], unsure_f[:, 0:GT], 0.0, None, ALU.is_gt, ALU.add,
                                                 accum_out=marked[:, GT:GT + 1]))
                    step(nc.vector.tensor_tensor(marked[:, 0:GT], marked[:, 0:GT], numbers[:], ALU.mult))
                    step(nc.vector.max(listed[:, 0:8], marked[:, 0:GT]))
                    step(nc.vector.match_replace(unsure_f[:, 0:GT], listed[:, 0:8], marked[:, 0:GT], 0.0))
                    step(nc.vector.max(listed[:, 8:16], unsure_f[:, 0:GT]))
                    step(nc.vector.tensor_copy(listed_i[:, 0:GT], listed[:]))
                    step(nc.vector.tensor_copy(listed_i[:, GT:GT + 1], marked[:, GT:GT + 1]))
                    dve.sem_clear(s_step)
                    tiles = dve.value_load(listed_i[0:1, GT:GT + 1], min_val=1, max_val=GT)
                    with dve.Fori(0, tiles) as k:
                        t = dve.value_load(listed_i[0:1, bass.ds(k, 1)], min_val=1, max_val=GT)
                        select_tile(slot, t - 1)
                dve.sem_inc(s_sel, 1)

            def probs(i, slot, n, jh):
                H = GH * i + n
                if jh == 0:
                    dve.wait_ge(s_exp, H + 1)
                    dve.wait_ge(s_T, at(H - 1))
                t = 2 * n + jh
                ins = nc.vector.scalar_tensor_tensor(p_sb[:, n % 2, jh, :], score_sb[:, slot, t, :], thr[:, slot, t:t + 1],
                                                     e_sb[:, n % 2, jh, :], ALU.is_ge, ALU.mult)
                if jh == 1:
                    ins.then_inc(s_P, 1)

            def invert(b):
                dve.wait_ge(s_Om, O_MOVES * (b + 1))
                dve.wait_ge(s_rd, at(16 * b))
                nc.vector.reciprocal(rec_sb[:], den_sb[:]).then_inc(s_rec, 1)

            def update_residual(b, p):
                dve.wait_ge(s_op, b + 1)
                dve.wait_ge(s_xg, b + 1)
                for t in range(TT):
                    ins = nc.vector.scalar_tensor_tensor(x_res[p][:, t, :], ps_x[:, t * E:(t + 1) * E], tg[:, 0:1],
                                                         x_res[p][:, t, :], ALU.mult, ALU.add)
                ins.then_inc(s_x1, 1)
                dve.wait_ge(s_x1, b + 1)
                moments(b, 1, x_res[p])

            def prepare_rounding(b):
                dve.wait_ge(s_xn[1], b + 1)
                dve.wait_ge(s_q, at(b))
                nc.vector.tensor_scalar(y_sb[:], xb_sb[:], rscl[:, 0:1], None, ALU.mult).then_inc(s_y, 1)
                dve.wait_ge(s_y, b + 1)
                exponent(magic_sb[:], y_sb[:]).then_inc(s_yb, 1)
                dve.wait_ge(s_yb, b + 1)
                magic(magic_sb[:]).then_inc(s_mg, 1)
                magnitude(yabs_sb[:], y_sb[:]).then_inc(s_nan, 1)
                dve.wait_ge(s_nan, 5 * b + 1)
                nc.vector.tensor_reduce(rowmax[:], yabs_sb[:], AX.X, ALU.max).then_inc(s_nan, 1)
                dve.wait_ge(s_nan, 5 * b + 2)
                nc.vector.tensor_scalar(nanrow[:], rowmax[:], 464.0, 3.0e38, ALU.is_gt, ALU.mult).then_inc(s_nan, 1)
                dve.wait_ge(s_nan, 5 * b + 3)
                nc.vector.tensor_scalar(nanrow[:], nanrow[:], 3.0e38, None, ALU.mult).then_inc(s_nan, 1)
                dve.wait_ge(s_nan, 5 * b + 4)
                nc.vector.tensor_tensor(rowmax[:], nanrow[:], nanrow[:], ALU.subtract).then_inc(s_nan, 1)

            def finish(b, p):
                dve.wait_ge(s_f, b + 1)
                dve.wait_ge(s_nan, 5 * b + 5)
                for t in range(TT):
                    ins = nc.vector.scalar_tensor_tensor(fbias_sb[:, t, :], f_sb[:, t, :], rowmax[:, t:t + 1], fb_row[:],
                                                         ALU.add, ALU.add)
                ins.then_inc(s_fb, 1)
                dve.wait_ge(s_fb, b + 1)
                nc.vector.scalar_tensor_tensor(x_res[p][:], fbias_sb[:], tg[:, 1:2], x_res[p][:],
                                               ALU.mult, ALU.add).then_inc(s_res, 1)

            front_moments(1)
            for i in range(2):
                for n in range(GH):
                    copy_scores(i, i, n, 0)
                    copy_scores(i, i, n, 1)
                if i == 0:
                    start_thresholds(0, 0)
            for r in range(GUIDES):
                guide_counts(0, 0, r)
                if r == GUIDES - 1:
                    start_thresholds(1, 1)
                for _ in update_thresholds(0, 0, r):
                    pass
                if r == 1:
                    front_moments(2)

            def batch(b, p, has):
                for g in range(2):
                    i = 2 * b + g
                    slot = 2 * p + g
                    ahead = (slot + 1) % RING
                    fresh = (slot + 2) % RING
                    mixed = (slot - 1) % RING
                    mixes = g == 1 or has(-1)
                    guided = g == 0 or has(1)
                    for r in range(GUIDES):
                        finals = final_tiles(i, slot, r)
                        next(finals)
                        if guided:
                            guide_counts(i + 1, ahead, r)
                        if r == 0 and mixes:
                            read_unsure(i - 1)
                        if has(1):
                            copy_scores(i + 2, fresh, 2 * r, 0)
                        next(finals)
                        if r == 0 and mixes:
                            convert_unsure(i - 1)
                        if has(1):
                            copy_scores(i + 2, fresh, 2 * r, 1)
                        next(finals, None)
                        if r == 0 and mixes:
                            settle(i - 1, mixed)
                        if r == 0:
                            masks, of, at_slot, first = has(-1), i - 2, fresh, GH - MASK_LAG
                        else:
                            masks, of, at_slot, first = mixes, i - 1, mixed, 2 * r - MASK_LAG
                        if masks:
                            for jh in range(2):
                                probs(of, at_slot, first, jh)
                        last = r == GUIDES - 1
                        if last and has(1):
                            for jh in range(2):
                                copy_scores(i + 2, fresh, 2 * r + 1, jh)
                            start_thresholds(i + 2, fresh)
                        steps = update_thresholds(i + 1, ahead, r) if guided else iter(())
                        ending = final_thresholds(i, slot) if last else iter(())
                        next(steps, None)
                        for jh in range(2):
                            next(ending, None)
                            if masks:
                                probs(of, at_slot, first + 1, jh)
                            next(steps, None)
                        for jh in range(2):
                            next(ending, None)
                            if has(1) and not last:
                                copy_scores(i + 2, fresh, 2 * r + 1, jh)
                            next(steps, None)
                        for _ in ending:
                            next(steps, None)
                        for _ in steps:
                            pass
                        if has(-3) and (g, r) == (0, 0):
                            prepare_rounding(b - 3)
                        if has(-2) and (g, r) == (0, 0):
                            invert(b - 2)
                        if has(-3) and (g, r) == (1, 0):
                            finish(b - 3, 1 - p)
                        if has(-2) and (g, r) == (1, 2):
                            update_residual(b - 2, p)
                        if has(3) and (g, r) == (1, 1):
                            front_moments(b + 3)

            schedule(dve, batch)
            read_unsure(2 * NB - 1)
            convert_unsure(2 * NB - 1)
            settle(2 * NB - 1, RING - 1)
            for n in range(GH - MASK_LAG, GH):
                for jh in range(2):
                    probs(2 * NB - 2, RING - 2, n, jh)
            prepare_rounding(NB - 3)
            invert(NB - 2)
            for n in range(GH):
                for jh in range(2):
                    probs(2 * NB - 1, RING - 1, n, jh)
            finish(NB - 3, 1)
            update_residual(NB - 2, 0)
            prepare_rounding(NB - 2)
            invert(NB - 1)
            finish(NB - 2, 0)
            update_residual(NB - 1, 1)
            prepare_rounding(NB - 1)
            finish(NB - 1, 1)


INS = ['x', 'ctx_1024', 'g_xattn', 'g_ffn', 'L0_xattn_Wq', 'L0_xattn_bq', 'L0_xattn_Wk', 'L0_xattn_bk', 'L0_xattn_Wv',
       'L0_xattn_bv', 'L0_xattn_Wo', 'L0_xattn_bo', 'L0_ffn_kernel', 'L0_ffn_input_scale', 'L0_ffn_kernel_scale',
       'L0_ffn_bias']


def kernel(**inputs):
    import numpy as _np
    import concourse.bacc as _bacc
    from concourse import mybir as _mybir
    from concourse.bass_utils import run_bass_kernel_spmd as _run

    nc = _bacc.Bacc("TRN2", target_bir_lowering=False, num_devices=1)
    arrays, args = {}, []
    for name in INS:
        a = _np.ascontiguousarray(inputs[name])
        arrays[f"in_{name}"] = a
        args.append(nc.dram_tensor(f"in_{name}", a.shape, _mybir.dt.from_np(a.dtype), kind="ExternalInput").ap())
    args.append(nc.dram_tensor("out_0", (NB, TOK, E), F32, kind="ExternalOutput").ap())
    build(nc, *args)
    r = _run(nc, [arrays], core_ids=[0])
    return r.results[0]["out_0"]
```
